# Optimizing a Trainium2 kernel written in Bass

```python
import numpy as np
import jax
import jax.numpy as jnp

def _softmax(x, axis=-1):
    return jax.nn.softmax(x, axis=axis)

def _gelu(x):
    return jax.nn.gelu(x, approximate=True)

def _silu(x):
    return jax.nn.silu(x)

def _sigmoid(x):
    return jax.nn.sigmoid(x)

def _layernorm(x, axis=-1, eps=1e-05):
    m = jnp.mean(x, axis=axis, keepdims=True)
    v = jnp.var(x, axis=axis, keepdims=True)
    return (x - m) / jnp.sqrt(v + eps)

def _scatter_add(tgt, idx, src, axis=0):
    return tgt.at[idx].add(src)

def _segment_sum(src, seg, n):
    return jax.ops.segment_sum(src, seg, n)
kernel_name = 'mk_adj_resnorm_d2_adj_r2_bd5b05'

def setup_inputs(seed: int=0):
    np.random.seed(seed)
    _w = jnp.asarray

    def _rec_inputs():
        import jax
        import jax.numpy as jnp
        _gk = jax.random.key(seed)
        x = -0.0005207 + 1.001 * jax.random.normal(jax.random.fold_in(_gk, 1), (8192, 128), jnp.float32)
        _w = (1.0 + jnp.arange(8192, dtype=jnp.float32)) ** (-0.5)
        _w = _w / _w.mean()
        _pij = jnp.clip(0.000488281 * _w[:, None] * _w[None, :], 0.0, 1.0)
        _a = jax.random.uniform(jax.random.fold_in(_gk, 2), (8192, 8192)) < _pij
        _a = jnp.logical_or(_a, jnp.eye(8192, dtype=bool))
        _af = _a.astype(jnp.float32)
        _af = _af * jax.random.uniform(jax.random.fold_in(_gk, 3), (8192, 8192), jnp.float32, 0.05, 1)
        adj = _af
        return (x, adj)
    x, adj = _rec_inputs()

    def _L0_gnn_setup():
        import jax, jax.numpy as jnp
        import numpy as np
        ALPHA = 0.1
        N, F = (8192, 128)
        key = jax.random.key(seed)
        k1, k2, k3 = jax.random.split(key, 3)
        x = jax.random.normal(k1, (N, F), dtype=jnp.float32)
        adj = jax.random.uniform(k2, (N, N), dtype=jnp.float32)
        h = jax.random.normal(k3, (N, F), dtype=jnp.float32)
        return {'x': x, 'adj': adj, 'h': h}
    _L0_gnn_all = _L0_gnn_setup()
    _L0_gnn_in = {k: v for k, v in _L0_gnn_all.items() if k in ('h',)}
    del _L0_gnn_all

    def _L1_gnn_setup():
        import jax, jax.numpy as jnp
        import numpy as np
        N, C_IN, C_OUT = (4096, 128, 128)
        BN_EPS = 1e-05
        EDGE_PROB = 0.004
        key = jax.random.key(seed)
        k1, k2, k3, k4, k5, k6 = jax.random.split(key, 6)
        node_features = jax.random.normal(k1, (N, C_IN), dtype=jnp.float32)
        adjacency_matrix = (jax.random.uniform(k2, (N, N)) < EDGE_PROB).astype(jnp.float32)
        s = 1.0 / np.sqrt(C_IN)
        W_n = jax.random.uniform(k3, (C_OUT, C_IN), jnp.float32, -s, s)
        b_n = jax.random.uniform(k4, (C_OUT,), jnp.float32, -s, s)
        W_c = jax.random.uniform(k5, (C_OUT, C_IN), jnp.float32, -s, s)
        b_c = jax.random.uniform(k6, (C_OUT,), jnp.float32, -s, s)
        gamma = jnp.ones((C_OUT,), jnp.float32)
        beta = jnp.zeros((C_OUT,), jnp.float32)
        return {'node_features': node_features, 'adjacency_matrix': adjacency_matrix, 'W_n': W_n, 'b_n': b_n, 'W_c': W_c, 'b_c': b_c, 'gamma': gamma, 'beta': beta}
    _L1_gnn_all = _L1_gnn_setup()
    _L1_gnn_in = {k: v for k, v in _L1_gnn_all.items() if k in ('W_n', 'b_n', 'W_c', 'b_c', 'gamma', 'beta')}
    del _L1_gnn_all
    return {'x': x, 'adj': adj, 'L0_gnn_h': _L0_gnn_in['h'], 'L1_gnn_W_n': _L1_gnn_in['W_n'], 'L1_gnn_b_n': _L1_gnn_in['b_n'], 'L1_gnn_W_c': _L1_gnn_in['W_c'], 'L1_gnn_b_c': _L1_gnn_in['b_c'], 'L1_gnn_gamma': _L1_gnn_in['gamma'], 'L1_gnn_beta': _L1_gnn_in['beta']}

def reference(x, adj, L0_gnn_h, L1_gnn_W_n, L1_gnn_b_n, L1_gnn_W_c, L1_gnn_b_c, L1_gnn_gamma, L1_gnn_beta):
    import jax
    import jax.numpy as jnp

    def _L0_gnn_ref(x, adj, h):
        import jax, jax.numpy as jnp
        import numpy as np
        ALPHA = 0.1
        N, F = (8192, 128)
        return (1.0 - ALPHA) * (adj @ x) + ALPHA * h

    def _L1_gnn_ref(node_features, adjacency_matrix, W_n, b_n, W_c, b_c, gamma, beta):
        import jax, jax.numpy as jnp
        import numpy as np
        N, C_IN, C_OUT = (4096, 128, 128)
        BN_EPS = 1e-05
        EDGE_PROB = 0.004
        deg = adjacency_matrix.sum(axis=1, keepdims=True)
        deg = jnp.where(deg == 0, jnp.ones_like(deg), deg)
        agg = adjacency_matrix.T @ node_features / deg
        h = agg @ W_n.T + b_n + node_features @ W_c.T + b_c
        mu = h.mean(axis=0)
        var = ((h - mu) ** 2).mean(axis=0)
        h_norm = (h - mu) * jax.lax.rsqrt(var + BN_EPS)
        return jax.nn.relu(gamma * h_norm + beta)
    x = _layernorm(x + _L0_gnn_ref(x, adj, L0_gnn_h), axis=-1)
    x = _layernorm(x + _L1_gnn_ref(x, adj, L1_gnn_W_n, L1_gnn_b_n, L1_gnn_W_c, L1_gnn_b_c, L1_gnn_gamma, L1_gnn_beta), axis=-1)
    return x

_drawn_inputs = setup_inputs


def setup_inputs(seed=0):
    import zlib

    import numpy as np

    out = dict(_drawn_inputs(seed))
    spreads = {'L1_gnn_gamma': (1.0, 0.2), 'L1_gnn_beta': (0.0, 0.1)}
    factors = {}
    for name, (base, spread) in spreads.items():
        noise = np.random.default_rng([zlib.crc32(name.encode()), seed]).standard_normal(out[name].shape)
        drawn = base * np.exp(spread * noise) if base else spread * noise
        out[name] = jnp.asarray(drawn.astype(out[name].dtype))
    for name, factor in factors.items():
        out[name] = (out[name] * factor).astype(out[name].dtype)
    return out
```

```python
import concourse.bass as bass
from concourse import mybir
from contextlib import ExitStack

FP32 = mybir.dt.float32
FP32R = mybir.dt.float32r
ALU = mybir.AluOpType
ACT = mybir.ActivationFunctionType
AX = mybir.AxisListType

P = 128
N = 8192
TILES = N // P
RB = 2
GROUPS = N // (RB * P)
CW = 512
CHUNKS = N // CW
CT = CW // P
HALVES = 2 * CHUNKS
EARLY = 7
SLOTS = CHUNKS + EARLY
LAG = 6
LEAD = 2
ALPHA = 0.1
LN_EPS = 1e-5
BN_EPS = 1e-5
W = RB * P

ORDER = list(range(EARLY, CHUNKS)) + list(range(EARLY))
LAST_ORDER = [c for c in ORDER if c != CHUNKS - 1] + [CHUNKS - 1]
NBUF = 3


def home(chunk, parity):
    return chunk + parity * CHUNKS if chunk < EARLY else chunk


def loads_before(chunk, g):
    return g // 2 + 1 if chunk < EARLY else g + 1


def adj_resnorm_kernel(nc, x, adj, h0, w_n, b_n, w_c, b_c, gamma, beta, out):
    x_v = x.rearrange("(t p) f -> p t f", p=P)
    h_v = h0.rearrange("(g r p) f -> g p r f", r=RB, p=P)
    adj_v = adj.rearrange("(g r p) n -> g p r n", r=RB, p=P)
    out_v = out.rearrange("(t p) f -> p t f", p=P)
    x1_dram = nc.dram_tensor("x1_scratch", (P, N), FP32, kind="Internal").ap()
    xc_dram = nc.dram_tensor("xc_scratch", (P, N), FP32, kind="Internal").ap()

    with ExitStack() as ctx:
        def sb(name, shape, dt=FP32):
            return ctx.enter_context(nc.sbuf_tensor(name, shape, dt))

        def pb(name):
            return ctx.enter_context(nc.psum_tensor(name, [P, CW], FP32))

        def sem(name):
            return ctx.enter_context(nc.semaphore(name))

        ring = sb("ring", [P, SLOTS, RB, CW])
        x_hi = sb("x_hi", [P, TILES, P], FP32R)
        x_lo = sb("x_lo", [P, TILES, P], FP32R)
        agg = sb("agg", [P, CHUNKS, CW])
        adjT = sb("adjT", [P, 2, 2, 2, W], FP32R)
        nat_hi = sb("nat_hi", [P, NBUF, CW], FP32R)
        nat_lo = sb("nat_lo", [P, NBUF, CW], FP32R)
        x1_hi = sb("x1_hi", [P, 2, RB, P], FP32R)
        x1_lo = sb("x1_lo", [P, 2, RB, P], FP32R)
        x1 = sb("x1", [P, RB, P])
        turned = sb("turned", [P, W])
        xc = sb("xc", [P, RB, P])
        hx = sb("hx", [P, RB, P])
        wT = sb("wT", [P, 2, P])
        bias = sb("bias", [P, P])
        ident = sb("ident", [P, P])
        part_deg = sb("part_deg", [P, 2, RB, CHUNKS])
        deg = sb("deg", [P, TILES])
        no_deg = sb("no_deg", [P, TILES])
        stats = sb("stats", [P, CT, 6])
        mv = sb("mv", [P, CT, 2])
        std = sb("std", [P, CT])
        bn_parts = sb("bn_parts", [P, CHUNKS, 6])
        bn_mv = sb("bn_mv", [P, 2])
        bn_scale = sb("bn_scale", [P, 1])
        bn_shift = sb("bn_shift", [P, 1])
        gb = sb("gb", [P, 2])
        eps = sb("eps", [P, 1])

        turn_ps = [pb("turn_ps0"), pb("turn_ps1")]
        row_ps = [pb("row_ps0"), pb("row_ps1")]
        agg_ps = [pb("agg_ps0"), pb("agg_ps1")]
        norm_ps = pb("norm_ps")
        xc_ps = pb("xc_ps")

        chunk_in = [sem(f"chunk_in{s}") for s in range(SLOTS)]
        x_in = [sem(f"x_in{s}") for s in range(EARLY)]
        small_in = sem("small_in")
        h_in = sem("h_in")
        x1_out = sem("x1_out")
        xc_moved = sem("xc_moved")
        tail_in = [sem(f"tail_in{q}") for q in range(CHUNKS)]
        rows_out = sem("rows_out")
        ident_zero = sem("ident_zero")
        ident_ready = sem("ident_ready")
        w_turned = sem("w_turned")
        bias_ready = sem("bias_ready")
        eps_ready = sem("eps_ready")
        x_hi_ready = sem("x_hi_ready")
        x_split = sem("x_split")
        turned_ps = sem("turned_ps")
        adjT_hi = sem("adjT_hi")
        adjT_lo = sem("adjT_lo")
        rows_mm = sem("rows_mm")
        nat_hi_ready = sem("nat_hi_ready")
        nat_lo_ready = sem("nat_lo_ready")
        nat_lo_dve = sem("nat_lo_dve")
        agg_mm = sem("agg_mm")
        agg_free = sem("agg_free")
        half_rows = sem("half_rows")
        rows_sum = sem("rows_sum")
        rows_nat = sem("rows_nat")
        hx_step = sem("hx_step")
        pre_ready = sem("pre_ready")
        norm_step = sem("norm_step")
        mv_ready = sem("mv_ready")
        std_ready = sem("std_ready")
        x1_ready = sem("x1_ready")
        x1_split = sem("x1_split")
        x1_turned = sem("x1_turned")
        x1_copied = sem("x1_copied")
        xc_mm = sem("xc_mm")
        xc_ps_read = sem("xc_ps_read")
        deg_ready = sem("deg_ready")
        deg_step = sem("deg_step")
        mix_mm = sem("mix_mm")
        h_ready = sem("h_ready")
        h_turned = sem("h_turned")
        hT_ready = sem("hT_ready")
        bn_part = sem("bn_part")
        bn_step = sem("bn_step")
        bn_std = sem("bn_std")
        relu_ready = sem("relu_ready")
        relu_turned = sem("relu_turned")
        y_ready = sem("y_ready")
        y_step = sem("y_step")
        y_mv = sem("y_mv")
        y_std = sem("y_std")
        y_rstd = sem("y_rstd")
        y_out = sem("y_out")

        block = ctx.enter_context(nc.Block())

        X_PIECE = 8
        X_PIECES = TILES // X_PIECE
        X_SLOT = CHUNKS
        LAST = GROUPS - 1

        def x_home(piece):
            return X_SLOT + piece % EARLY

        def x_staged(piece):
            return ring[:, x_home(piece), :, :].rearrange("p r n -> p (r n)").rearrange("p (t f) -> p t f", f=P)

        def tail_home(q):
            return home(q, (LAST + 1) % 2) if q < EARLY else home(ORDER[q - EARLY], LAST % 2)

        def tail_x1(q):
            return ring[:, tail_home(q), 0, :]

        def tail_xc(q):
            return ring[:, tail_home(q), 1, :]

        @block.sync
        def _(sp):
            def load_chunk(g, chunk, parity):
                cols = slice(chunk * CW, (chunk + 1) * CW)
                src = adj_v[g, :, :, cols] if isinstance(g, int) else adj_v[bass.ds(g, 1), :, :, cols].squeeze(0)
                slot = home(chunk, parity)
                sp.dma_start(ring[:, slot, :, :], src).then_inc(chunk_in[slot], 16)

            def load_x(piece):
                sp.dma_start(x_staged(piece), x_v[:, piece * X_PIECE:(piece + 1) * X_PIECE, :])\
                  .then_inc(x_in[piece % EARLY], 16)

            load_x(0)
            load_chunk(0, 0, 0)
            load_chunk(0, 1, 0)
            sp.dma_start(xc[:, 0, :], w_c).then_inc(small_in, 16)
            sp.dma_start(xc[:, 1, :], w_n).then_inc(xc_moved, 16)
            sp.dma_start(bias[:, :], b_n.partition_broadcast(P)).then_inc(small_in, 16)
            sp.dma_start(turned[:, 0:P], b_c.partition_broadcast(P)).then_inc(small_in, 16)
            sp.dma_start(gb[:, 0:1], gamma.rearrange("(p a) -> p a", a=1)).then_inc(small_in, 16)
            sp.dma_start(gb[:, 1:2], beta.rearrange("(p a) -> p a", a=1)).then_inc(small_in, 16)
            sp.dma_start(hx[:, :, :], h_v[0]).then_inc(h_in, 16)
            for piece in range(1, X_PIECES):
                if piece >= EARLY:
                    sp.wait_ge(x_split, piece - EARLY + 1)
                load_x(piece)
                load_chunk(0, 2 * piece, 0)
                load_chunk(0, 2 * piece + 1, 0)
            for c in range(EARLY):
                sp.wait_ge(x_split, (c + EARLY if c + EARLY < X_PIECES else c) + 1)
                load_chunk(1, c, 1)

            def freed(g, p):
                sp.wait_ge(nat_lo_ready, HALVES * (g - 1) + 2 * p + 2)

            def small_traffic(g, p):
                if p == 0:
                    sp.wait_ge(x1_ready, g)
                    sp.dma_start(x1_dram[:, bass.ds((g - 1) * W, W)], x1[:, :, :].rearrange("p r f -> p (r f)"))\
                      .then_inc(x1_out, 16)
                if p == 4:
                    sp.wait_ge(xc_ps_read, g + 1)
                    sp.dma_start(xc_dram[:, bass.ds((g - 1) * W, W)], xc[:, :, :].rearrange("p r f -> p (r f)"))\
                      .then_inc(xc_moved, 16)

            def load_h(g):
                sp.wait_ge(pre_ready, g)
                src = h_v[g] if isinstance(g, int) else h_v[bass.ds(g, 1), :, :, :].squeeze(0)
                sp.dma_start(hx[:, :, :], src).then_inc(h_in, 16)

            def group(g, parity):
                for p in range(CHUNKS):
                    freed(g, p)
                    if p < CHUNKS - EARLY:
                        load_chunk(g, ORDER[p], parity)
                    elif not isinstance(g, int) or g < LAST:
                        load_chunk(g + 1, ORDER[p], 1 - parity)
                    small_traffic(g, p)
                    if p == 0:
                        load_h(g)

            with sp.Fori(0, (LAST - 1) // 2) as k:
                group(2 * k + 1, 1)
                group(2 * k + 2, 0)
            group(LAST, 1)

            small_traffic(GROUPS, 0)
            small_traffic(GROUPS, 4)
            sp.wait_ge(x1_out, 16 * GROUPS)
            sp.wait_ge(xc_moved, 16 * (GROUPS + 1))
            for q in range(CHUNKS):
                if q >= EARLY:
                    sp.wait_ge(nat_lo_ready, HALVES * LAST + q - EARLY + 1)
                    sp.wait_ge(nat_lo_dve, q - EARLY + 1)
                cols = slice(LAST_ORDER[q] * CW, (LAST_ORDER[q] + 1) * CW)
                sp.dma_start(tail_x1(q), x1_dram[:, cols]).then_inc(tail_in[q], 16)
                sp.dma_start(tail_xc(q), xc_dram[:, cols]).then_inc(tail_in[q], 16)
            for q in range(CHUNKS):
                sp.wait_ge(y_out, q + 1)
                c = LAST_ORDER[q]
                sp.dma_start(out_v[:, c * CT:(c + 1) * CT, :],
                             tail_x1(q).rearrange("p (t f) -> p t f", f=P)).then_inc(rows_out, 16)
            sp.wait_ge(rows_out, 16 * CHUNKS)

        @block.gpsimd
        def _(pool):
            pool.memset(ident[:, :], 0.0).then_inc(ident_zero, 1)
            pool.wait_ge(ident_zero, 1)
            pool.affine_select(out=ident[:, :], in_=ident[:, :], compare_op=ALU.not_equal, fill=1.0,
                               base=0, pattern=[[-1, P]], channel_multiplier=1).then_inc(ident_ready, 1)
            for i in range(2):
                pool.memset(agg[:, i * CHUNKS // 2:(i + 1) * CHUNKS // 2, :], 0.0).then_inc(agg_free, 1)

            def low_part(g, m, parity):
                slot, r, b = home(ORDER[m // 2], parity), m % 2, m % NBUF
                pool.wait_ge(nat_hi_ready, HALVES * g + m + 1)
                pool.tensor_tensor(nat_lo[:, b, :], ring[:, slot, r, :], nat_hi[:, b, :].bitcast(FP32),
                                   ALU.subtract).then_inc(nat_lo_ready, 1)

            for m in range(LEAD):
                low_part(0, m, 0)

            def group(g, parity):
                for s in range(HALVES):
                    m = s + LEAD
                    if m < HALVES:
                        low_part(g - 1, m, 1 - parity)
                    else:
                        low_part(g, m - HALVES, parity)

            with pool.Fori(0, (LAST - 1) // 2) as k:
                group(2 * k + 1, 1)
                group(2 * k + 2, 0)
            for m in range(LEAD, HALVES):
                low_part(LAST - 1, m, 0)
            for m in range(0, HALVES, 2):
                low_part(LAST, m, LAST % 2)

        @block.scalar
        def _(act):
            def turn_high(g, idx):
                act.wait_ge(turned_ps, HALVES * g + idx + 1)
                if not (isinstance(g, int) and g == 0 and idx < 2):
                    act.wait_ge(rows_mm, HALVES * g + idx - 1)
                act.activation(adjT[:, idx % 2, :, 0, :],
                               turn_ps[idx % 2][:, :].rearrange("p (t w) -> p t w", w=W), ACT.Copy)\
                   .then_inc(adjT_hi, 1)

            def nat_high(g, m, parity, first=False):
                slot, r, b = home(ORDER[m // 2], parity), m % 2, m % NBUF
                if m >= NBUF:
                    act.wait_ge(agg_mm, HALVES * g + m - NBUF + 1)
                elif m < LEAD and not first:
                    act.wait_ge(agg_mm, HALVES * (g - 1) + HALVES - 1 + m)
                    if m == 0:
                        act.wait_ge(deg_ready, g)
                act.activation(nat_hi[:, b, :], ring[:, slot, r, :], ACT.Copy,
                               accum_out=part_deg[:, parity, r, m // 2:m // 2 + 1]).then_inc(nat_hi_ready, 1)

            def half_of_rows(g, parity):
                act.wait_ge(rows_mm, HALVES * (g + 1))
                if not (isinstance(g, int) and g == 0):
                    act.wait_ge(xc_mm, g)
                else:
                    act.wait_ge(bias_ready, 1)
                act.activation(turned[:, :], row_ps[parity][:, W:2 * W], ACT.Copy).then_inc(half_rows, 1)

            def row_std(g):
                act.wait_ge(mv_ready, RB * (g + 1))
                act.activation(std[:, 0:RB], mv[:, 0:RB, 1], ACT.Sqrt, bias=eps[:, 0:1]).then_inc(std_ready, 1)

            def copy_x1T(g):
                act.wait_ge(x1_turned, g)
                act.activation(turned[:, :], norm_ps[:, W:2 * W], ACT.Copy).then_inc(x1_copied, 1)

            act.wait_ge(eps_ready, 1)
            for s in range(HALVES + LAG + LEAD):
                if s == HALVES + LEAD:
                    half_of_rows(0, 0)
                if s == HALVES + LEAD + 2:
                    row_std(0)
                turn_high(s // HALVES, s % HALVES)
                if s >= HALVES + LAG:
                    nat_high(0, s - HALVES - LAG, 0, first=True)

            def group(g, parity):
                for s in range(HALVES):
                    if s == 1:
                        copy_x1T(g)
                    if s == HALVES - LAG:
                        half_of_rows(g, parity)
                    if s == HALVES - LAG + 2:
                        row_std(g)
                    idx = s + LAG + LEAD
                    if idx < HALVES:
                        turn_high(g, idx)
                    elif not isinstance(g, int) or g < LAST:
                        turn_high(g + 1, idx - HALVES)
                    m = s + LEAD
                    if m < HALVES:
                        nat_high(g - 1, m, 1 - parity)
                    else:
                        nat_high(g, m - HALVES, parity)

            with act.Fori(0, (LAST - 1) // 2) as k:
                group(2 * k + 1, 1)
                group(2 * k + 2, 0)
            group(LAST, 1)

            def copy_hT(q):
                act.wait_ge(h_turned, q + 1)
                act.activation(agg[:, LAST_ORDER[q], :], turn_ps[q % 2][:, :], ACT.Copy).then_inc(hT_ready, 1)

            for p in range(CHUNKS + 4):
                if p == 1:
                    copy_x1T(GROUPS)
                for m in (2 * p + LEAD, 2 * p + LEAD + 1):
                    if m < HALVES:
                        nat_high(LAST, m, 1)
                if p >= 4:
                    copy_hT(p - 4)
            act.wait_ge(bn_step, 1)
            act.activation(bn_scale[:, :], bn_mv[:, 1:2], ACT.Sqrt, bias=eps[:, 0:1]).then_inc(bn_std, 1)
            act.wait_ge(bn_step, 5)
            for q in range(CHUNKS + 1):
                if q < CHUNKS:
                    c = LAST_ORDER[q]
                    act.activation(agg[:, c, :], agg[:, c, :], ACT.Relu, scale=bn_scale[:, 0:1],
                                   bias=bn_shift[:, 0:1]).then_inc(relu_ready, 1)
                if q >= 1:
                    act.wait_ge(y_mv, q)
                    act.activation(std[:, :], mv[:, :, 1], ACT.Sqrt, bias=eps[:, 0:1]).then_inc(y_std, 1)

        @block.vector
        def _(dve):
            dve.memset(deg[:, :], 0.0).then_inc(deg_ready, 1)
            dve.memset(eps[:, :], LN_EPS).then_inc(eps_ready, 1)

            def split_x(piece):
                rows = slice(piece * X_PIECE, (piece + 1) * X_PIECE)
                dve.wait_ge(x_in[piece % EARLY], 16 * (piece // EARLY + 1))
                dve.tensor_copy(x_hi[:, rows, :], x_staged(piece)).then_inc(x_hi_ready, 1)
                dve.wait_ge(x_hi_ready, piece + 1)
                dve.tensor_tensor(x_lo[:, rows, :], x_staged(piece), x_hi[:, rows, :].bitcast(FP32),
                                  ALU.subtract).then_inc(x_split, 1)

            def turn_low(g, idx):
                dve.wait_ge(adjT_hi, HALVES * g + idx + 1)
                dve.tensor_tensor(adjT[:, idx % 2, :, 1, :],
                                  turn_ps[idx % 2][:, :].rearrange("p (t w) -> p t w", w=W),
                                  adjT[:, idx % 2, :, 0, :].bitcast(FP32), ALU.subtract).then_inc(adjT_lo, 1)

            def add_agg(g, p):
                dve.wait_ge(agg_mm, HALVES * g + 2 * p + 2)
                c = ORDER[p]
                dve.tensor_tensor(agg[:, c, :], agg_ps[p % 2][:, :], agg[:, c, :], ALU.add).then_inc(agg_free, 1)

            def add_hx(g):
                dve.wait_ge(h_in, 16 * (g + 1))
                tiles = slice(0, RB) if isinstance(g, int) and g == 0 else bass.ds(g * RB, RB)
                dve.scalar_tensor_tensor(hx[:, :, :], hx[:, :, :], ALPHA, x_hi[:, tiles, :].bitcast(FP32),
                                         ALU.mult, ALU.add).then_inc(hx_step, 1)
                dve.wait_ge(hx_step, 2 * g + 1)
                dve.tensor_tensor(hx[:, :, :], hx[:, :, :], x_lo[:, tiles, :].bitcast(FP32), ALU.add)\
                   .then_inc(hx_step, 1)

            def sum_rows(g, parity):
                dve.wait_ge(half_rows, g + 1)
                dve.tensor_tensor(turned[:, :], row_ps[parity][:, 0:W], turned[:, :], ALU.add)\
                   .then_inc(rows_sum, 1)

            def row_stats(g):
                dve.wait_ge(rows_nat, g + 1)
                dve.wait_ge(hx_step, 2 * g + 2)
                if not (isinstance(g, int) and g == 0):
                    dve.wait_ge(x1_out, 16 * g)
                    dve.wait_ge(x1_turned, g)
                dve.scalar_tensor_tensor(x1[:, :, :].rearrange("p r f -> p (r f)"), norm_ps[:, 0:W], 1.0 - ALPHA,
                                         hx[:, :, :].rearrange("p r f -> p (r f)"), ALU.mult, ALU.add)\
                   .then_inc(pre_ready, 1)
                dve.wait_ge(pre_ready, g + 1)
                for r in range(RB):
                    dve.bn_stats(stats[:, r, :], x1[:, r, :]).then_inc(norm_step, 1)

            def row_aggr(g):
                for r in range(RB):
                    dve.bn_aggr(mv[:, r, :], stats[:, r, :]).then_inc(mv_ready, 1)

            def normalise(g, parity):
                dve.wait_ge(std_ready, g + 1)
                dve.reciprocal(std[:, 0:RB], std[:, 0:RB]).then_inc(norm_step, 1)
                dve.wait_ge(norm_step, 4 * g + 3)
                for r in range(RB):
                    op = dve.tensor_scalar(x1[:, r, :], x1[:, r, :], mv[:, r, 0:1], std[:, r:r + 1],
                                           ALU.subtract, ALU.mult)
                op.then_inc(x1_ready, 1)
                dve.wait_ge(x1_ready, g + 1)
                dve.tensor_copy(x1_hi[:, parity, :, :], x1[:, :, :]).then_inc(norm_step, 1)
                dve.wait_ge(norm_step, 4 * g + 4)
                dve.tensor_tensor(x1_lo[:, parity, :, :], x1[:, :, :], x1_hi[:, parity, :, :].bitcast(FP32),
                                  ALU.subtract).then_inc(x1_split, 1)

            def add_bias(g):
                dve.wait_ge(xc_mm, g)
                dve.wait_ge(xc_moved, 16 * g)
                dve.tensor_tensor(xc[:, :, :], xc_ps[:, 0:W].rearrange("p (r f) -> p r f", f=P),
                                  bias[:, :].unsqueeze(1).to_broadcast([P, RB, P]), ALU.add).then_inc(xc_ps_read, 1)

            def sum_deg(g, parity):
                dve.wait_ge(nat_hi_ready, HALVES * g)
                tiles = slice((g - 1) * RB, g * RB) if isinstance(g, int) else bass.ds((g - 1) * RB, RB)
                dve.reduce_sum(deg[:, tiles], part_deg[:, 1 - parity, :, :], AX.X).then_inc(deg_ready, 1)

            split_x(0)
            split_x(1)
            for s in range(HALVES + LAG + LEAD):
                if s == 2:
                    dve.wait_ge(small_in, 16 * 5)
                    dve.tensor_tensor(bias[:, :], bias[:, :], turned[:, 0:P], ALU.add).then_inc(bias_ready, 1)
                    dve.wait_ge(w_turned, 1)
                    dve.tensor_copy(wT[:, :, :], xc_ps[:, 0:W].rearrange("p (r f) -> p r f", f=P))\
                       .then_inc(xc_ps_read, 1)
                if s == 12:
                    add_hx(0)
                if s % 4 == 3 and s // 4 + 2 < X_PIECES:
                    split_x(s // 4 + 2)
                if s == HALVES + LEAD:
                    sum_rows(0, 0)
                if s == HALVES + LEAD + 1:
                    row_stats(0)
                    dve.wait_ge(norm_step, 2)
                if s == HALVES + LEAD + 3:
                    normalise(0, 0)
                turn_low(s // HALVES, s % HALVES)
                if s == HALVES + LEAD + 1:
                    row_aggr(0)

            def group(g, parity):
                for s in range(HALVES):
                    if s == 4:
                        add_bias(g)
                    if s == 10:
                        add_hx(g)
                    if s == HALVES - LAG:
                        sum_rows(g, parity)
                    if s == HALVES - LAG + 1:
                        row_stats(g)
                        dve.wait_ge(norm_step, 4 * g + 2)
                    if s == HALVES - LAG + 3:
                        normalise(g, parity)
                    idx = s + LAG + LEAD
                    if idx < HALVES:
                        turn_low(g, idx)
                    elif not isinstance(g, int) or g < LAST:
                        turn_low(g + 1, idx - HALVES)
                    if s == HALVES - LAG + 1:
                        row_aggr(g)
                    if s % 2 == 1:
                        add_agg(g - 1, s // 2)
                sum_deg(g, parity)

            with dve.Fori(0, (LAST - 1) // 2) as k:
                group(2 * k + 1, 1)
                group(2 * k + 2, 0)
            group(LAST, 1)

            steps = [0]

            def invert_deg(cols):
                d = deg[:, cols]
                z = no_deg[:, cols]
                dve.tensor_scalar(z, d, 0.0, None, ALU.is_equal).then_inc(deg_step, 1)
                dve.wait_ge(deg_step, steps[0] + 1)
                dve.tensor_tensor(d, d, z, ALU.add).then_inc(deg_step, 1)
                dve.wait_ge(deg_step, steps[0] + 2)
                dve.reciprocal(d, d).then_inc(deg_step, 1)
                dve.wait_ge(deg_step, steps[0] + 3)
                steps[0] += 3

            def h_rows(q):
                c = LAST_ORDER[q]
                dve.wait_ge(mix_mm, q + 1)
                dve.wait_ge(tail_in[q], 32)
                for t in range(CT):
                    cols = slice(t * P, (t + 1) * P)
                    op = dve.scalar_tensor_tensor(tail_xc(q)[:, cols], row_ps[q % 2][:, cols],
                                                  deg[:, c * CT + t:c * CT + t + 1], tail_xc(q)[:, cols],
                                                  ALU.mult, ALU.add)
                op.then_inc(h_ready, 1)

            def bn_part_of(q):
                dve.wait_ge(hT_ready, q + 1)
                dve.bn_stats(bn_parts[:, q, :], agg[:, LAST_ORDER[q], :]).then_inc(bn_part, 1)

            dve.wait_ge(deg_ready, 1 + LAST)
            invert_deg(slice(0, TILES - RB))
            for p in range(CHUNKS + 4):
                if p < CHUNKS:
                    m = 2 * p + 1
                    slot, b = home(ORDER[p], LAST % 2), m % NBUF
                    dve.wait_ge(nat_hi_ready, HALVES * LAST + m + 1)
                    dve.tensor_tensor(nat_lo[:, b, :], ring[:, slot, 1, :], nat_hi[:, b, :].bitcast(FP32),
                                      ALU.subtract).then_inc(nat_lo_dve, 1)
                    if p >= 1:
                        add_agg(LAST, p - 1)
                if p == CHUNKS:
                    add_agg(LAST, CHUNKS - 1)
                    sum_deg(GROUPS, GROUPS % 2)
                    dve.wait_ge(deg_ready, 1 + GROUPS)
                    invert_deg(slice(TILES - RB, TILES))
                if p == 2:
                    add_bias(GROUPS)
                if 3 <= p < CHUNKS + 3:
                    h_rows(p - 3)
                if p >= 4:
                    bn_part_of(p - 4)

            dve.wait_ge(bn_part, CHUNKS)
            dve.bn_aggr(bn_mv[:, :], bn_parts[:, :, :]).then_inc(bn_step, 1)
            dve.wait_ge(bn_std, 1)
            dve.reciprocal(bn_scale[:, :], bn_scale[:, :]).then_inc(bn_step, 1)
            dve.wait_ge(bn_step, 2)
            dve.tensor_tensor(bn_scale[:, :], bn_scale[:, :], gb[:, 0:1], ALU.mult).then_inc(bn_step, 1)
            dve.wait_ge(bn_step, 3)
            dve.tensor_tensor(bn_shift[:, :], bn_mv[:, 0:1], bn_scale[:, :], ALU.mult).then_inc(bn_step, 1)
            dve.wait_ge(bn_step, 4)
            dve.tensor_tensor(bn_shift[:, :], gb[:, 1:2], bn_shift[:, :], ALU.subtract).then_inc(bn_step, 1)

            for q in range(CHUNKS + 1):
                if q >= 1:
                    dve.wait_ge(y_std, q)
                    dve.reciprocal(std[:, :], std[:, :]).then_inc(y_rstd, 1)
                    dve.wait_ge(y_rstd, q)
                    for t in range(CT):
                        cols = slice(t * P, (t + 1) * P)
                        op = dve.tensor_scalar(tail_x1(q - 1)[:, cols], tail_x1(q - 1)[:, cols],
                                               mv[:, t, 0:1], std[:, t:t + 1], ALU.subtract, ALU.mult)
                    op.then_inc(y_out, 1)
                if q < CHUNKS:
                    dve.wait_ge(relu_turned, q + 1)
                    dve.tensor_tensor(tail_x1(q), row_ps[q % 2][:, :], tail_x1(q), ALU.add).then_inc(y_ready, 1)
                    dve.wait_ge(y_ready, q + 1)
                    for t in range(CT):
                        dve.bn_stats(stats[:, t, :], tail_x1(q)[:, t * P:(t + 1) * P]).then_inc(y_step, 1)
                    dve.wait_ge(y_step, CT * (q + 1))
                    if q >= 1:
                        dve.wait_ge(y_out, q)
                    for t in range(CT):
                        op = dve.bn_aggr(mv[:, t, :], stats[:, t, :])
                    op.then_inc(y_mv, 1)

        @block.tensor
        def _(pe):
            def turn(g, idx, parity):
                chunk, half = idx // 2, idx % 2
                slot = home(chunk, parity)
                if idx % 2 == 0:
                    if isinstance(g, int):
                        pe.wait_ge(chunk_in[slot], 16 * loads_before(chunk, g))
                    elif chunk < EARLY:
                        pe.wait_ge(chunk_in[slot], (g - parity) * 8 + 16)
                    else:
                        pe.wait_ge(chunk_in[slot], g * 16 + 16)
                if not (isinstance(g, int) and g == 0 and idx < 2):
                    pe.wait_ge(adjT_lo, HALVES * g + idx - 1)
                for t in range(2):
                    for r in range(RB):
                        col = (2 * half + t) * P
                        op = pe.transpose(turn_ps[idx % 2][:, t * W + r * P:t * W + (r + 1) * P],
                                          ring[:, slot, r, col:col + P], ident[:, :])
                op.then_inc(turned_ps, 1)

            def rows(g, idx, parity):
                pe.wait_ge(adjT_lo, HALVES * g + idx + 1)
                if idx == 0 and not (isinstance(g, int) and g < 2):
                    pe.wait_ge(rows_sum, g - 1)
                for t in range(2):
                    tile = 2 * idx + t
                    first, last = idx == 0 and t == 0, idx == HALVES - 1 and t == 1
                    pe.matmul(row_ps[parity][:, :], x_hi[:, tile, :],
                              adjT[:, idx % 2, t, :, :].rearrange("p a w -> p (a w)"), start=first, stop=False,
                              skip_group_check=True)
                    op = pe.matmul(row_ps[parity][:, 0:W], x_lo[:, tile, :], adjT[:, idx % 2, t, 0, :],
                                   start=False, stop=last, skip_group_check=True)
                op.then_inc(rows_mm, 1)

            def aggregate(g, m, parity, split_elsewhere=False):
                p, r, b = m // 2, m % 2, m % NBUF
                if m == 0:
                    pe.wait_ge(x1_split, g + 1)
                if split_elsewhere and r == 1:
                    pe.wait_ge(nat_lo_dve, p + 1)
                elif split_elsewhere:
                    pe.wait_ge(nat_lo_ready, HALVES * g + p + 1)
                else:
                    pe.wait_ge(nat_lo_ready, HALVES * g + m + 1)
                if r == 0:
                    pe.wait_ge(agg_free, CHUNKS * g + p + 1)
                bank = agg_ps[p % 2][:, :]
                pe.matmul(bank, x1_hi[:, parity, r, :], nat_hi[:, b, :], start=r == 0, stop=False)
                pe.matmul(bank, x1_lo[:, parity, r, :], nat_hi[:, b, :], start=False, stop=False)
                pe.matmul(bank, x1_hi[:, parity, r, :], nat_lo[:, b, :], start=False, stop=r == RB - 1)\
                  .then_inc(agg_mm, 1)

            def turn_rows(g):
                pe.wait_ge(rows_sum, g + 1)
                for r in range(RB):
                    op = pe.transpose(norm_ps[:, r * P:(r + 1) * P], turned[:, r * P:(r + 1) * P], ident[:, :])
                op.then_inc(rows_nat, 1)

            def turn_x1(g):
                pe.wait_ge(x1_ready, g)
                for r in range(RB):
                    op = pe.transpose(norm_ps[:, W + r * P:W + (r + 1) * P], x1[:, r, :], ident[:, :])
                op.then_inc(x1_turned, 1)

            def mix_x1(g):
                pe.wait_ge(x1_copied, g)
                pe.wait_ge(xc_ps_read, g)
                for r in range(RB):
                    op = pe.matmul(xc_ps[:, r * P:(r + 1) * P], turned[:, r * P:(r + 1) * P], wT[:, 0, :],
                                   start=True, stop=True)
                op.then_inc(xc_mm, 1)

            pe.wait_ge(ident_ready, 1)
            turn(0, 0, 0)
            turn(0, 1, 0)
            pe.wait_ge(small_in, 16 * 5)
            pe.wait_ge(xc_moved, 16)
            for i in range(2):
                op = pe.transpose(xc_ps[:, i * P:(i + 1) * P], xc[:, i, :], ident[:, :])
            op.then_inc(w_turned, 1)
            for s in range(HALVES + LAG):
                nxt = s + LEAD
                turn(nxt // HALVES, nxt % HALVES, nxt // HALVES)
                if s == 0:
                    pe.wait_ge(xc_ps_read, 1)
                if s < HALVES and s % 4 == 0:
                    pe.wait_ge(x_split, s // 4 + 1)
                rows(s // HALVES, s % HALVES, s // HALVES)
                if s == HALVES:
                    turn_rows(0)

            def group(g, parity):
                for s in range(HALVES):
                    more = not isinstance(g, int) or g < LAST
                    nxt = s + LAG + LEAD
                    if nxt < HALVES:
                        turn(g, nxt, parity)
                    elif more:
                        turn(g + 1, nxt - HALVES, 1 - parity)
                    now = s + LAG
                    if now < HALVES:
                        rows(g, now, parity)
                    elif more:
                        rows(g + 1, now - HALVES, 1 - parity)
                    aggregate(g - 1, s, 1 - parity)
                    if s == 0:
                        turn_x1(g)
                    if s == 2:
                        mix_x1(g)
                    if s == HALVES - LAG:
                        turn_rows(g)

            with pe.Fori(0, (LAST - 1) // 2) as k:
                group(2 * k + 1, 1)
                group(2 * k + 2, 0)
            group(LAST, 1)

            def mix_agg(q):
                c = LAST_ORDER[q]
                pe.wait_ge(agg_free, 2 + CHUNKS * LAST + ORDER.index(c) + 1)
                if q >= 2:
                    pe.wait_ge(h_ready, q - 1)
                for t in range(CT):
                    op = pe.matmul(row_ps[q % 2][:, t * P:(t + 1) * P], agg[:, c, t * P:(t + 1) * P], wT[:, 1, :],
                                   start=True, stop=True)
                op.then_inc(mix_mm, 1)

            def turn_h(q):
                pe.wait_ge(h_ready, q + 1)
                if q >= 2:
                    pe.wait_ge(hT_ready, q - 1)
                for t in range(CT):
                    op = pe.transpose(turn_ps[q % 2][:, t * P:(t + 1) * P], tail_xc(q)[:, t * P:(t + 1) * P],
                                      ident[:, :])
                op.then_inc(h_turned, 1)

            for p in range(CHUNKS + 4):
                if p == 1:
                    turn_x1(GROUPS)
                if p == 2:
                    mix_x1(GROUPS)
                if p < CHUNKS:
                    aggregate(LAST, 2 * p, LAST % 2, split_elsewhere=True)
                    aggregate(LAST, 2 * p + 1, LAST % 2, split_elsewhere=True)
                if 2 <= p < CHUNKS + 2:
                    mix_agg(p - 2)
                if 3 <= p < CHUNKS + 3:
                    turn_h(p - 3)

            for q in range(CHUNKS):
                pe.wait_ge(relu_ready, q + 1)
                if q >= 2:
                    pe.wait_ge(y_ready, q - 1)
                c = LAST_ORDER[q]
                for t in range(CT):
                    op = pe.transpose(row_ps[q % 2][:, t * P:(t + 1) * P], agg[:, c, t * P:(t + 1) * P], ident[:, :])
                op.then_inc(relu_turned, 1)


_INS = ['x', 'adj', 'L0_gnn_h', 'L1_gnn_W_n', 'L1_gnn_b_n', 'L1_gnn_W_c', 'L1_gnn_b_c', 'L1_gnn_gamma',
        'L1_gnn_beta']


def kernel(**inputs):
    import numpy as _np
    import concourse.bacc as _bacc
    from concourse import mybir as _mybir
    from concourse.bass_utils import run_bass_kernel_spmd as _run

    nc = _bacc.Bacc("TRN2", target_bir_lowering=False, num_devices=1, dynamic_dma_scratch_size=2048)
    arrays, args = {}, []
    for name in _INS:
        a = _np.ascontiguousarray(inputs[name])
        arrays[f"in_{name}_dram"] = a
        args.append(nc.dram_tensor(f"in_{name}_dram", a.shape, _mybir.dt.from_np(a.dtype), kind="ExternalInput").ap())
    args.append(nc.dram_tensor("out_0_dram", (N, P), _mybir.dt.float32, kind="ExternalOutput").ap())
    adj_resnorm_kernel(nc, *args)
    r = _run(nc, [arrays], core_ids=[0])
    return r.results[0]["out_0_dram"]
```

```python
import concourse.bass as bass
from concourse import mybir
from contextlib import ExitStack

FP32 = mybir.dt.float32
FP32R = mybir.dt.float32r
ALU = mybir.AluOpType
ACT = mybir.ActivationFunctionType
AX = mybir.AxisListType

P = 128
N = 8192
TILES = N // P
RB = 2
GROUPS = N // (RB * P)
CW = 512
CHUNKS = N // CW
CT = CW // P
HALVES = 2 * CHUNKS
EARLY = 6
SLOTS = CHUNKS + EARLY
QHOMES = 2
Q = 32
LAG = 5
LEAD = 2
ALPHA = 0.1
LN_EPS = 1e-5
BN_EPS = 1e-5
W = RB * P

ORDER = list(range(EARLY, CHUNKS)) + list(range(EARLY))
LAST_ORDER = [c for c in ORDER if c != CHUNKS - 1] + [CHUNKS - 1]
X_CUTS = [0, 2, 8, CHUNKS]
NBUF = 3




def by_vector(g, chunk):
    return chunk % 2 == 1 and not (isinstance(g, int) and g == 0)


def home(chunk, parity):
    return chunk + parity * CHUNKS if chunk < EARLY else chunk


def loads_before(chunk, g):
    return g // 2 + 1 if chunk < EARLY else g + 1


def adj_resnorm_kernel(nc, x, adj, h0, w_n, b_n, w_c, b_c, gamma, beta, out):
    x_v = x.rearrange("(g r p) f -> g p r f", r=RB, p=P)
    x_q = x.rearrange("(c k u) f -> k c (u f)", k=P, u=CT)
    adj_q = adj.rearrange("(g i a) (c q n) -> g c q a i n", a=Q, i=W // Q, q=4, n=P)
    h_v = h0.rearrange("(g r p) f -> g p r f", r=RB, p=P)
    adj_v = adj.rearrange("(g r p) n -> g p r n", r=RB, p=P)
    out_v = out.rearrange("(t p) f -> p t f", p=P)
    x1_dram = nc.dram_tensor("x1_scratch", (P, N), FP32, kind="Internal").ap()
    xc_dram = nc.dram_tensor("xc_scratch", (P, N), FP32, kind="Internal").ap()

    with ExitStack() as ctx:
        def sb(name, shape, dt=FP32):
            return ctx.enter_context(nc.sbuf_tensor(name, shape, dt))

        def pb(name):
            return ctx.enter_context(nc.psum_tensor(name, [P, CW], FP32))

        def sem(name):
            return ctx.enter_context(nc.semaphore(name))

        ring = sb("ring", [P, SLOTS + QHOMES, RB, CW])
        x_hi = sb("x_hi", [P, TILES, P], FP32R)
        x_lo = sb("x_lo", [P, TILES, P], FP32R)
        agg = sb("agg", [P, CHUNKS, CW])
        adjT = sb("adjT", [P, 2, 2, 2, W], FP32R)
        nat_hi = sb("nat_hi", [P, NBUF, CW], FP32R)
        nat_lo = sb("nat_lo", [P, NBUF, CW], FP32R)
        x1_hi = sb("x1_hi", [P, 2, RB, P], FP32R)
        x1_lo = sb("x1_lo", [P, 2, RB, P], FP32R)
        x1 = sb("x1", [P, RB, P])
        turned = sb("turned", [P, W])
        xc = sb("xc", [P, RB, P])
        hx = sb("hx", [P, RB, P])
        w_cT = sb("w_cT", [P, P])
        ident = sb("ident", [P, P])
        part_deg = sb("part_deg", [P, 2, RB, CHUNKS])
        deg = sb("deg", [P, TILES])
        stats = sb("stats", [P, CT, 6])
        mv = sb("mv", [P, CT, 2])
        std = sb("std", [P, RB])
        bn_mv = sb("bn_mv", [P, 2])
        bn_scale = sb("bn_scale", [P, 1])
        bn_shift = sb("bn_shift", [P, 1])
        by_feature = sb("by_feature", [P, 4])
        bn_parts = ring[:, SLOTS, 0, 0:CHUNKS * 6].rearrange("p (c s) -> p c s", s=6)
        no_deg = ring[:, SLOTS + 1, 0, 0:TILES]
        scale_y = ring[:, SLOTS, 1, 0:2 * CT].rearrange("p (b t) -> p b t", t=CT)
        shift_y = ring[:, SLOTS + 1, 1, 0:2 * CT].rearrange("p (b t) -> p b t", t=CT)
        w_n_in, w_nT = hx[:, 0, :], hx[:, 1, :]
        eps = sb("eps", [P, 1])

        turn_ps = [pb("turn_ps0"), pb("turn_ps1")]
        row_ps = [pb("row_ps0"), pb("row_ps1")]
        agg_ps = [pb("agg_ps0"), pb("agg_ps1")]
        norm_ps = pb("norm_ps")
        xc_ps = pb("xc_ps")

        chunk_in = [sem(f"chunk_in{s}") for s in range(SLOTS)]
        quarter_in = [sem(f"quarter_in{s}") for s in range(QHOMES)]
        x_in = [sem(f"x_in{s}") for s in range(len(X_CUTS) - 1)]
        small_in = sem("small_in")
        res_in = sem("res_in")
        w_n_here = sem("w_n_here")
        w_n_turned = sem("w_n_turned")
        w_n_ready = sem("w_n_ready")
        h_in = sem("h_in")
        x1_out = sem("x1_out")
        xc_out = sem("xc_out")
        tail_in = [sem(f"tail_in{q}") for q in range(CHUNKS)]
        rows_out = sem("rows_out")
        ident_zero = sem("ident_zero")
        ident_ready = sem("ident_ready")
        w_turned = sem("w_turned")
        bias_ready = sem("bias_ready")
        eps_ready = sem("eps_ready")
        x_hi_ready = sem("x_hi_ready")
        x_split = sem("x_split")
        turned_ps = sem("turned_ps")
        turned_dve = sem("turned_dve")
        adjT_hi = sem("adjT_hi")
        adjT_lo = sem("adjT_lo")
        rows_mm = sem("rows_mm")
        nat_hi_ready = sem("nat_hi_ready")
        nat_lo_ready = sem("nat_lo_ready")
        nat_lo_dve = sem("nat_lo_dve")
        agg_mm = sem("agg_mm")
        agg_free = sem("agg_free")
        half_rows = sem("half_rows")
        rows_sum = sem("rows_sum")
        rows_nat = sem("rows_nat")
        hx_step = sem("hx_step")
        pre_ready = sem("pre_ready")
        norm_step = sem("norm_step")
        mv_ready = sem("mv_ready")
        std_ready = sem("std_ready")
        x1_ready = sem("x1_ready")
        x1_split = sem("x1_split")
        x1_turned = sem("x1_turned")
        x1_copied = sem("x1_copied")
        xc_mm = sem("xc_mm")
        xc_ps_read = sem("xc_ps_read")
        deg_ready = sem("deg_ready")
        deg_step = sem("deg_step")
        mix_mm = sem("mix_mm")
        h_ready = sem("h_ready")
        h_turned = sem("h_turned")
        hT_ready = sem("hT_ready")
        bn_part = sem("bn_part")
        bn_step = sem("bn_step")
        bn_std = sem("bn_std")
        relu_ready = sem("relu_ready")
        relu_turned = sem("relu_turned")
        y_ready = sem("y_ready")
        y_step = sem("y_step")
        y_mv = sem("y_mv")
        y_std = sem("y_std")
        y_rstd = sem("y_rstd")
        y_shift = sem("y_shift")
        y_out_act = sem("y_out_act")
        y_out_pool = sem("y_out_pool")

        block = ctx.enter_context(nc.Block())

        LAST = GROUPS - 1
        X_SLOT = CHUNKS
        assert (EARLY + QHOMES) * RB * CW == TILES * P

        def x_staged(chunk):
            half = ring[:, X_SLOT + chunk // 2, chunk % 2, :]
            return half.rearrange("p (t f) -> p t f", f=P)

        def quarters(h):
            return ring[:, SLOTS + h, :, :].rearrange("p r n -> p (r n)").rearrange("p (i n) -> p i n", n=P)

        def turns_before(g, chunk):
            if isinstance(g, int) and g == 0:
                return 2 * chunk
            if by_vector(g, chunk):
                return CHUNKS * (g - 1) + chunk - 1
            return HALVES + CHUNKS * (g - 1) + chunk

        def low_by_dve(m):
            return m % 8 == 5

        def low_by_dve_until(p):
            return sum(low_by_dve(m) for m in range(2 * p + 2))

        def tail_home(q):
            return home(q, (LAST + 1) % 2) if q < EARLY else home(ORDER[q - EARLY], LAST % 2)

        def tail_x1(q):
            return ring[:, tail_home(q), 0, :]

        def tail_xc(q):
            return ring[:, tail_home(q), 1, :]

        @block.sync
        def _(sp):
            def load_chunk(g, chunk, parity):
                cols = slice(chunk * CW, (chunk + 1) * CW)
                src = adj_v[g, :, :, cols] if isinstance(g, int) else adj_v[bass.ds(g, 1), :, :, cols].squeeze(0)
                slot = home(chunk, parity)
                sp.dma_start(ring[:, slot, :, :], src).then_inc(chunk_in[slot], 16)

            def load_quarters(g, chunk):
                h = chunk // 2 % QHOMES
                for q in range(4):
                    src = adj_q[g, chunk, q] if isinstance(g, int) else \
                        adj_q[bass.ds(g, 1), chunk, q, :, :, :].squeeze(0)
                    sp.dma_start(quarters(h)[q * Q:(q + 1) * Q, :, :], src).then_inc(quarter_in[h], 16)

            def load_residual(g):
                src = x_v[g] if isinstance(g, int) else x_v[bass.ds(g, 1), :, :, :].squeeze(0)
                sp.dma_start(xc[:, :, :], src).then_inc(res_in, 16)

            load_chunk(0, 0, 0)
            load_chunk(0, 1, 0)
            sp.dma_start(xc[:, 0, :], w_c).then_inc(small_in, 16)
            for i, v in enumerate((gamma, beta, b_n, b_c)):
                sp.dma_start(by_feature[:, i:i + 1], v.rearrange("(p a) -> p a", a=1)).then_inc(small_in, 16)
            sp.dma_start(hx[:, :, :], h_v[0]).then_inc(h_in, 16)
            for c in range(2, CHUNKS):
                load_chunk(0, c, 0)
                if c == 8:
                    sp.wait_ge(w_turned, 1)
                    load_residual(0)
            for c in range(EARLY):
                sp.wait_ge(x_split, 2 * c + 2)
                load_chunk(1, c, 1)
            for n, c in enumerate((1, 3, 5)):
                if n < QHOMES:
                    sp.wait_ge(x_split, 2 * (EARLY + n) + 2)
                else:
                    sp.wait_ge(turned_dve, 2)
                load_quarters(1, c)

            def freed(g, p):
                sp.wait_ge(nat_lo_ready, HALVES * (g - 1) + 2 * p + 2)

            def small_traffic(g, p):
                if p == 0:
                    sp.wait_ge(x1_ready, g)
                    sp.dma_start(x1_dram[:, bass.ds((g - 1) * W, W)], x1[:, :, :].rearrange("p r f -> p (r f)"))\
                      .then_inc(x1_out, 16)
                if p == 3:
                    sp.wait_ge(xc_ps_read, g + 1)
                    sp.dma_start(xc_dram[:, bass.ds((g - 1) * W, W)], xc[:, :, :].rearrange("p r f -> p (r f)"))\
                      .then_inc(xc_out, 16)

            def load_h(g):
                sp.wait_ge(pre_ready, g)
                src = h_v[g] if isinstance(g, int) else h_v[bass.ds(g, 1), :, :, :].squeeze(0)
                sp.dma_start(hx[:, :, :], src).then_inc(h_in, 16)

            def group(g, parity):
                for p in range(CHUNKS):
                    freed(g, p)
                    if p < CHUNKS - EARLY:
                        load_chunk(g, ORDER[p], parity)
                    elif not isinstance(g, int) or g < LAST:
                        load_chunk(g + 1, ORDER[p], 1 - parity)
                    if p % 2 == 0:
                        n, c = p // 2 + 3, p + 7
                        if c < CHUNKS:
                            sp.wait_ge(turned_dve, CHUNKS * (g - 1) + 2 * n - 2)
                            load_quarters(g, c)
                        elif not isinstance(g, int) or g < LAST:
                            sp.wait_ge(turned_dve, CHUNKS * (g - 1) + 2 * n - 2)
                            load_quarters(g + 1, c - CHUNKS)
                    small_traffic(g, p)
                    if p == 0:
                        load_h(g)
                    if p == 6:
                        sp.wait_ge(xc_out, 16 * g)
                        load_residual(g)

            with sp.Fori(0, (LAST - 1) // 2) as k:
                group(2 * k + 1, 1)
                group(2 * k + 2, 0)
            group(LAST, 1)

            sp.wait_ge(pre_ready, GROUPS)
            sp.dma_start(w_n_in, w_n).then_inc(w_n_here, 16)
            small_traffic(GROUPS, 0)
            small_traffic(GROUPS, 3)
            sp.wait_ge(x1_out, 16 * GROUPS)
            sp.wait_ge(xc_out, 16 * GROUPS)
            for q in range(CHUNKS):
                if q >= EARLY:
                    by_dve = low_by_dve_until(q - EARLY)
                    sp.wait_ge(nat_lo_ready, HALVES * LAST + 2 * (q - EARLY + 1) - by_dve)
                    if by_dve:
                        sp.wait_ge(nat_lo_dve, by_dve)
                cols = slice(LAST_ORDER[q] * CW, (LAST_ORDER[q] + 1) * CW)
                sp.dma_start(tail_x1(q), x1_dram[:, cols]).then_inc(tail_in[q], 16)
                sp.dma_start(tail_xc(q), xc_dram[:, cols]).then_inc(tail_in[q], 16)
            for q in range(CHUNKS):
                sp.wait_ge(y_out_act, q + 1)
                sp.wait_ge(y_out_pool, q + 1)
                c = LAST_ORDER[q]
                sp.dma_start(out_v[:, c * CT:(c + 1) * CT, :],
                             tail_x1(q).rearrange("p (t f) -> p t f", f=P)).then_inc(rows_out, 16)
            sp.wait_ge(rows_out, 16 * CHUNKS)

        @block.gpsimd
        def _(pool):
            pool.memset(ident[:, :], 0.0).then_inc(ident_zero, 1)
            pool.wait_ge(ident_zero, 1)
            pool.affine_select(out=ident[:, :], in_=ident[:, :], compare_op=ALU.not_equal, fill=1.0,
                               base=0, pattern=[[-1, P]], channel_multiplier=1).then_inc(ident_ready, 1)
            for i in range(2):
                pool.memset(agg[:, i * CHUNKS // 2:(i + 1) * CHUNKS // 2, :], 0.0).then_inc(agg_free, 1)

            def low_part(g, m, parity):
                slot, r, b = home(ORDER[m // 2], parity), m % 2, m % NBUF
                pool.wait_ge(nat_hi_ready, HALVES * g + m + 1)
                pool.tensor_tensor(nat_lo[:, b, :], ring[:, slot, r, :], nat_hi[:, b, :].bitcast(FP32),
                                   ALU.subtract).then_inc(nat_lo_ready, 1)

            for m in range(LEAD):
                low_part(0, m, 0)

            def group(g, parity):
                for s in range(HALVES):
                    m = s + LEAD
                    if m < HALVES:
                        low_part(g - 1, m, 1 - parity)
                    else:
                        low_part(g, m - HALVES, parity)

            with pool.Fori(0, (LAST - 1) // 2) as k:
                group(2 * k + 1, 1)
                group(2 * k + 2, 0)
            for m in range(LEAD, HALVES):
                low_part(LAST - 1, m, 0)
            for m in range(HALVES):
                if not low_by_dve(m):
                    low_part(LAST, m, LAST % 2)
            for q in range(CHUNKS):
                pool.wait_ge(y_shift, q + 1)
                for t in range(CT // 2, CT):
                    cols = slice(t * P, (t + 1) * P)
                    op = pool.tensor_scalar(tail_x1(q)[:, cols], tail_x1(q)[:, cols], scale_y[:, q % 2, t:t + 1],
                                            shift_y[:, q % 2, t:t + 1], ALU.mult, ALU.add)
                op.then_inc(y_out_pool, 1)

        @block.scalar
        def _(act):
            def turn_high(g, idx):
                act.wait_ge(turned_dve if by_vector(g, idx // 2) else turned_ps,
                            turns_before(g, idx // 2) + idx % 2 + 1)
                if not (isinstance(g, int) and g == 0 and idx < 2):
                    act.wait_ge(rows_mm, HALVES * g + idx - 1)
                act.activation(adjT[:, idx % 2, :, 0, :],
                               turn_ps[idx % 2][:, :].rearrange("p (t w) -> p t w", w=W), ACT.Copy)\
                   .then_inc(adjT_hi, 1)

            def nat_high(g, m, parity, first=False):
                slot, r, b = home(ORDER[m // 2], parity), m % 2, m % NBUF
                if m >= NBUF:
                    act.wait_ge(agg_mm, HALVES * g + m - NBUF + 1)
                elif m < LEAD and not first:
                    act.wait_ge(agg_mm, HALVES * (g - 1) + HALVES - 1 + m)
                    if m == 0:
                        act.wait_ge(deg_ready, g)
                act.activation(nat_hi[:, b, :], ring[:, slot, r, :], ACT.Copy,
                               accum_out=part_deg[:, parity, r, m // 2:m // 2 + 1]).then_inc(nat_hi_ready, 1)

            def half_of_rows(g, parity):
                act.wait_ge(rows_mm, HALVES * (g + 1))
                if not (isinstance(g, int) and g == 0):
                    act.wait_ge(xc_mm, g)
                act.activation(turned[:, :], row_ps[parity][:, W:2 * W], ACT.Copy).then_inc(half_rows, 1)

            def row_std(g):
                act.wait_ge(mv_ready, RB * (g + 1))
                act.activation(std[:, 0:RB], mv[:, 0:RB, 1], ACT.Sqrt, bias=eps[:, 0:1]).then_inc(std_ready, 1)

            def copy_x1T(g):
                act.wait_ge(x1_turned, g)
                act.activation(turned[:, :], norm_ps[:, W:2 * W], ACT.Copy).then_inc(x1_copied, 1)

            staged = ring[:, X_SLOT:, :, :].rearrange("p s r n -> p (s r) n")
            for i, (first, end) in enumerate(zip(X_CUTS, X_CUTS[1:])):
                act.dma_start(staged[:, first:end, :], x_q[:, first:end, :]).then_inc(x_in[i], 16)
            act.wait_ge(eps_ready, 1)
            for s in range(HALVES + LAG + LEAD):
                if s == HALVES + LEAD + 2:
                    row_std(0)
                turn_high(s // HALVES, s % HALVES)
                if s >= HALVES + LAG:
                    nat_high(0, s - HALVES - LAG, 0, first=True)
                if s == HALVES + LEAD - 1:
                    half_of_rows(0, 0)

            def group(g, parity):
                for s in range(HALVES):
                    if s == 1:
                        copy_x1T(g)
                    if s == HALVES - LAG + 2:
                        row_std(g)
                    m = s + LEAD
                    if m < HALVES:
                        nat_high(g - 1, m, 1 - parity)
                    else:
                        nat_high(g, m - HALVES, parity)
                    idx = s + LAG + LEAD
                    if idx < HALVES:
                        turn_high(g, idx)
                    elif not isinstance(g, int) or g < LAST:
                        turn_high(g + 1, idx - HALVES)
                    if s == HALVES - LAG - 1:
                        half_of_rows(g, parity)

            with act.Fori(0, (LAST - 1) // 2) as k:
                group(2 * k + 1, 1)
                group(2 * k + 2, 0)
            group(LAST, 1)

            def copy_hT(q):
                act.wait_ge(h_turned, q + 1)
                act.activation(agg[:, LAST_ORDER[q], :], turn_ps[q % 2][:, :], ACT.Identity,
                               bias=by_feature[:, 2:3]).then_inc(hT_ready, 1)

            act.wait_ge(bias_ready, 1)
            for p in range(CHUNKS + 4):
                if p == 1:
                    copy_x1T(GROUPS)
                for m in (2 * p + LEAD, 2 * p + LEAD + 1):
                    if m < HALVES:
                        nat_high(LAST, m, 1)
                if p >= 4:
                    copy_hT(p - 4)
            act.wait_ge(bn_step, 1)
            act.activation(bn_scale[:, :], bn_mv[:, 1:2], ACT.Sqrt, bias=eps[:, 0:1]).then_inc(bn_std, 1)
            act.wait_ge(bn_step, 5)
            for q in range(CHUNKS + 1):
                if q < CHUNKS:
                    c = LAST_ORDER[q]
                    act.activation(agg[:, c, :], agg[:, c, :], ACT.Relu, scale=bn_scale[:, 0:1],
                                   bias=bn_shift[:, 0:1]).then_inc(relu_ready, 1)
                if q >= 1:
                    act.wait_ge(y_mv, q)
                    b = (q - 1) % 2
                    if q >= 3:
                        act.wait_ge(y_out_pool, q - 2)
                        act.wait_ge(y_out_act, q - 2)
                    act.activation(scale_y[:, b, :], mv[:, :, 1], ACT.Sqrt, bias=eps[:, 0:1]).then_inc(y_std, 1)
                    act.wait_ge(y_shift, q)
                    for t in range(CT // 2):
                        cols = slice(t * P, (t + 1) * P)
                        op = act.activation(tail_x1(q - 1)[:, cols], tail_x1(q - 1)[:, cols], ACT.Identity,
                                            scale=scale_y[:, b, t:t + 1], bias=shift_y[:, b, t:t + 1])
                    op.then_inc(y_out_act, 1)

        @block.vector
        def _(dve):
            dve.memset(deg[:, :], 0.0).then_inc(deg_ready, 1)
            dve.memset(eps[:, :], LN_EPS).then_inc(eps_ready, 1)

            def split_x(c):
                tiles = slice(c * CT, (c + 1) * CT)
                dve.wait_ge(x_in[sum(c >= cut for cut in X_CUTS[1:])], 16)
                dve.tensor_copy(x_hi[:, tiles, :], x_staged(c)).then_inc(x_hi_ready, 1)
                dve.wait_ge(x_hi_ready, c + 1)
                dve.tensor_tensor(x_lo[:, tiles, :], x_staged(c), x_hi[:, tiles, :].bitcast(FP32),
                                  ALU.subtract).then_inc(x_split, 1)

            def turn_quarters(g, idx):
                chunk, half = idx // 2, idx % 2
                h = chunk // 2 % QHOMES
                if half == 0:
                    dve.wait_ge(quarter_in[h], 64 * (4 * (g - 1) + chunk // 4 + 1))
                dve.wait_ge(adjT_lo, HALVES * g + idx - 1)
                for t in range(2):
                    u = 2 * half + t
                    op = dve.transpose(turn_ps[idx % 2][:, t * W:(t + 1) * W], quarters(h)[:, :, u::CT])
                op.then_inc(turned_dve, 1)

            def turn_low(g, idx):
                dve.wait_ge(adjT_hi, HALVES * g + idx + 1)
                dve.tensor_tensor(adjT[:, idx % 2, :, 1, :],
                                  turn_ps[idx % 2][:, :].rearrange("p (t w) -> p t w", w=W),
                                  adjT[:, idx % 2, :, 0, :].bitcast(FP32), ALU.subtract).then_inc(adjT_lo, 1)

            def add_agg(g, p):
                dve.wait_ge(agg_mm, HALVES * g + 2 * p + 2)
                c = ORDER[p]
                dve.tensor_tensor(agg[:, c, :], agg_ps[p % 2][:, :], agg[:, c, :], ALU.add).then_inc(agg_free, 1)

            def add_hx(g):
                dve.wait_ge(h_in, 16 * (g + 1))
                dve.wait_ge(res_in, 16 * (g + 1))
                dve.scalar_tensor_tensor(hx[:, :, :], hx[:, :, :], ALPHA, xc[:, :, :], ALU.mult, ALU.add)\
                   .then_inc(hx_step, 1)

            def sum_rows(g, parity):
                dve.wait_ge(half_rows, g + 1)
                dve.tensor_tensor(turned[:, :], row_ps[parity][:, 0:W], turned[:, :], ALU.add)\
                   .then_inc(rows_sum, 1)

            def row_stats(g):
                dve.wait_ge(rows_nat, g + 1)
                dve.wait_ge(hx_step, g + 1)
                if not (isinstance(g, int) and g == 0):
                    dve.wait_ge(x1_out, 16 * g)
                    dve.wait_ge(x1_turned, g)
                dve.scalar_tensor_tensor(x1[:, :, :].rearrange("p r f -> p (r f)"), norm_ps[:, 0:W], 1.0 - ALPHA,
                                         hx[:, :, :].rearrange("p r f -> p (r f)"), ALU.mult, ALU.add)\
                   .then_inc(pre_ready, 1)
                dve.wait_ge(pre_ready, g + 1)
                for r in range(RB):
                    dve.bn_stats(stats[:, r, :], x1[:, r, :]).then_inc(norm_step, 1)

            def row_aggr(g):
                for r in range(RB):
                    dve.bn_aggr(mv[:, r, :], stats[:, r, :]).then_inc(mv_ready, 1)

            def normalise(g, parity):
                dve.wait_ge(std_ready, g + 1)
                dve.reciprocal(std[:, 0:RB], std[:, 0:RB]).then_inc(norm_step, 1)
                dve.wait_ge(norm_step, 4 * g + 3)
                for r in range(RB):
                    op = dve.tensor_scalar(x1[:, r, :], x1[:, r, :], mv[:, r, 0:1], std[:, r:r + 1],
                                           ALU.subtract, ALU.mult)
                op.then_inc(x1_ready, 1)

            def split_x1(g, parity):
                dve.wait_ge(x1_ready, g + 1)
                dve.tensor_copy(x1_hi[:, parity, :, :], x1[:, :, :]).then_inc(norm_step, 1)
                dve.wait_ge(norm_step, 4 * g + 4)
                dve.tensor_tensor(x1_lo[:, parity, :, :], x1[:, :, :], x1_hi[:, parity, :, :].bitcast(FP32),
                                  ALU.subtract).then_inc(x1_split, 1)

            def copy_xc(g):
                dve.wait_ge(xc_mm, g)
                dve.tensor_copy(xc[:, :, :], xc_ps[:, 0:W].rearrange("p (r f) -> p r f", f=P))\
                   .then_inc(xc_ps_read, 1)

            def sum_deg(g, parity):
                dve.wait_ge(nat_hi_ready, HALVES * g)
                tiles = slice((g - 1) * RB, g * RB) if isinstance(g, int) else bass.ds((g - 1) * RB, RB)
                dve.reduce_sum(deg[:, tiles], part_deg[:, 1 - parity, :, :], AX.X).then_inc(deg_ready, 1)

            split_x(0)
            for s in range(HALVES + LAG + LEAD):
                if s == 2:
                    dve.wait_ge(small_in, 16 * 5)
                    dve.tensor_tensor(by_feature[:, 2:3], by_feature[:, 2:3], by_feature[:, 3:4], ALU.add)\
                       .then_inc(bias_ready, 1)
                    dve.wait_ge(w_turned, 1)
                    dve.tensor_copy(w_cT[:, :], xc_ps[:, 0:P]).then_inc(xc_ps_read, 1)
                if s == HALVES - 8:
                    add_hx(0)
                if s % 2 == 0 and s // 2 + 1 < CHUNKS:
                    split_x(s // 2 + 1)
                nxt = s + 1
                if nxt < HALVES + LAG + LEAD + 1 and by_vector(nxt // HALVES, nxt % HALVES // 2):
                    turn_quarters(nxt // HALVES, nxt % HALVES)
                if s == HALVES + LEAD + 1:
                    dve.wait_ge(norm_step, 2)
                turn_low(s // HALVES, s % HALVES)
                if s == HALVES + LEAD - 1:
                    sum_rows(0, 0)
                if s == HALVES + LEAD:
                    row_stats(0)
                if s == HALVES + LEAD + 1:
                    row_aggr(0)
                if s == HALVES + LEAD + 2:
                    normalise(0, 0)
                if s == HALVES + LEAD + 3:
                    split_x1(0, 0)

            def group(g, parity):
                for s in range(HALVES):
                    if s == 4:
                        copy_xc(g)
                    if s == HALVES - 12:
                        add_hx(g)
                    nxt = s + LAG + LEAD + 1
                    if nxt < HALVES:
                        if by_vector(g, nxt // 2):
                            turn_quarters(g, nxt)
                    elif (not isinstance(g, int) or g < LAST) and by_vector(g + 1, (nxt - HALVES) // 2):
                        turn_quarters(g + 1, nxt - HALVES)
                    if s == HALVES - LAG + 1:
                        dve.wait_ge(norm_step, 4 * g + 2)
                    idx = s + LAG + LEAD
                    if idx < HALVES:
                        turn_low(g, idx)
                    elif not isinstance(g, int) or g < LAST:
                        turn_low(g + 1, idx - HALVES)
                    if s % 2 == 1:
                        add_agg(g - 1, s // 2)
                    if s == HALVES - LAG - 1:
                        sum_rows(g, parity)
                    if s == HALVES - LAG:
                        row_stats(g)
                    if s == HALVES - LAG + 1:
                        row_aggr(g)
                    if s == HALVES - LAG + 2:
                        normalise(g, parity)
                    if s == HALVES - LAG + 3:
                        split_x1(g, parity)
                sum_deg(g, parity)

            with dve.Fori(0, (LAST - 1) // 2) as k:
                group(2 * k + 1, 1)
                group(2 * k + 2, 0)
            group(LAST, 1)

            steps = [0]

            def invert_deg(cols):
                d = deg[:, cols]
                z = no_deg[:, cols]
                dve.tensor_scalar(z, d, 0.0, None, ALU.is_equal).then_inc(deg_step, 1)
                dve.wait_ge(deg_step, steps[0] + 1)
                dve.tensor_tensor(d, d, z, ALU.add).then_inc(deg_step, 1)
                dve.wait_ge(deg_step, steps[0] + 2)
                dve.reciprocal(d, d).then_inc(deg_step, 1)
                dve.wait_ge(deg_step, steps[0] + 3)
                steps[0] += 3

            def h_rows(q):
                c = LAST_ORDER[q]
                dve.wait_ge(mix_mm, q + 1)
                dve.wait_ge(tail_in[q], 32)
                for t in range(CT):
                    cols = slice(t * P, (t + 1) * P)
                    op = dve.scalar_tensor_tensor(tail_xc(q)[:, cols], row_ps[q % 2][:, cols],
                                                  deg[:, c * CT + t:c * CT + t + 1], tail_xc(q)[:, cols],
                                                  ALU.mult, ALU.add)
                op.then_inc(h_ready, 1)

            def bn_part_of(q):
                dve.wait_ge(hT_ready, q + 1)
                dve.bn_stats(bn_parts[:, q, :], agg[:, LAST_ORDER[q], :]).then_inc(bn_part, 1)

            dve.wait_ge(deg_ready, 1 + LAST)
            invert_deg(slice(0, TILES - RB))
            for p in range(CHUNKS + 4):
                if p == 0:
                    dve.wait_ge(w_n_turned, 1)
                    dve.tensor_copy(w_nT, xc_ps[:, W:W + P]).then_inc(w_n_ready, 1)
                for m in (2 * p, 2 * p + 1):
                    if m < HALVES and low_by_dve(m):
                        slot, b = home(ORDER[p], LAST % 2), m % NBUF
                        dve.wait_ge(nat_hi_ready, HALVES * LAST + m + 1)
                        dve.tensor_tensor(nat_lo[:, b, :], ring[:, slot, m % 2, :], nat_hi[:, b, :].bitcast(FP32),
                                          ALU.subtract).then_inc(nat_lo_dve, 1)
                if 1 <= p <= CHUNKS:
                    add_agg(LAST, p - 1)
                if p == CHUNKS:
                    sum_deg(GROUPS, GROUPS % 2)
                    dve.wait_ge(deg_ready, 1 + GROUPS)
                    invert_deg(slice(TILES - RB, TILES))
                if p == 2:
                    copy_xc(GROUPS)
                if 3 <= p < CHUNKS + 3:
                    h_rows(p - 3)
                if p >= 4:
                    bn_part_of(p - 4)

            dve.wait_ge(bn_part, CHUNKS)
            dve.bn_aggr(bn_mv[:, :], bn_parts[:, :, :]).then_inc(bn_step, 1)
            dve.wait_ge(bn_std, 1)
            dve.reciprocal(bn_scale[:, :], bn_scale[:, :]).then_inc(bn_step, 1)
            dve.wait_ge(bn_step, 2)
            dve.tensor_tensor(bn_scale[:, :], bn_scale[:, :], by_feature[:, 0:1], ALU.mult).then_inc(bn_step, 1)
            dve.wait_ge(bn_step, 3)
            dve.tensor_tensor(bn_shift[:, :], bn_mv[:, 0:1], bn_scale[:, :], ALU.mult).then_inc(bn_step, 1)
            dve.wait_ge(bn_step, 4)
            dve.tensor_tensor(bn_shift[:, :], by_feature[:, 1:2], bn_shift[:, :], ALU.subtract).then_inc(bn_step, 1)

            for q in range(CHUNKS + 1):
                if q < CHUNKS:
                    dve.wait_ge(relu_turned, q + 1)
                    dve.tensor_tensor(tail_x1(q), row_ps[q % 2][:, :], tail_x1(q), ALU.add).then_inc(y_ready, 1)
                if q >= 1:
                    b = (q - 1) % 2
                    dve.wait_ge(y_std, q)
                    dve.reciprocal(scale_y[:, b, :], scale_y[:, b, :]).then_inc(y_rstd, 1)
                    dve.wait_ge(y_rstd, q)
                    if q >= 3:
                        dve.wait_ge(y_out_pool, q - 2)
                        dve.wait_ge(y_out_act, q - 2)
                    dve.scalar_tensor_tensor(shift_y[:, b, :], mv[:, :, 0], -1.0, scale_y[:, b, :], ALU.mult, ALU.mult)\
                       .then_inc(y_shift, 1)
                if q < CHUNKS:
                    dve.wait_ge(y_ready, q + 1)
                    for t in range(CT):
                        dve.bn_stats(stats[:, t, :], tail_x1(q)[:, t * P:(t + 1) * P]).then_inc(y_step, 1)
                    if q >= 1:
                        dve.wait_ge(y_shift, q)
                    dve.wait_ge(y_step, CT * (q + 1))
                    for t in range(CT):
                        op = dve.bn_aggr(mv[:, t, :], stats[:, t, :])
                    op.then_inc(y_mv, 1)

        @block.tensor
        def _(pe):
            def turn(g, idx, parity):
                chunk, half = idx // 2, idx % 2
                if by_vector(g, chunk):
                    return
                slot = home(chunk, parity)
                tiles = ring[:, slot, :, :].rearrange("p r (k u) -> p r u k", u=CT)
                if idx % 2 == 0:
                    if isinstance(g, int):
                        pe.wait_ge(chunk_in[slot], 16 * loads_before(chunk, g))
                    elif chunk < EARLY:
                        pe.wait_ge(chunk_in[slot], (g - parity) * 8 + 16)
                    else:
                        pe.wait_ge(chunk_in[slot], g * 16 + 16)
                if not (isinstance(g, int) and g == 0 and idx < 2):
                    pe.wait_ge(adjT_lo, HALVES * g + idx - 1)
                for t in range(2):
                    for r in range(RB):
                        op = pe.transpose(turn_ps[idx % 2][:, t * W + r * P:t * W + (r + 1) * P],
                                          tiles[:, r, 2 * half + t, :], ident[:, :])
                op.then_inc(turned_ps, 1)

            def rows(g, idx, parity):
                pe.wait_ge(adjT_lo, HALVES * g + idx + 1)
                if idx == 0 and not (isinstance(g, int) and g < 2):
                    pe.wait_ge(rows_sum, g - 1)
                for t in range(2):
                    tile = 2 * idx + t
                    first, last = idx == 0 and t == 0, idx == HALVES - 1 and t == 1
                    pe.matmul(row_ps[parity][:, :], x_hi[:, tile, :],
                              adjT[:, idx % 2, t, :, :].rearrange("p a w -> p (a w)"), start=first, stop=False,
                              skip_group_check=True)
                    op = pe.matmul(row_ps[parity][:, 0:W], x_lo[:, tile, :], adjT[:, idx % 2, t, 0, :],
                                   start=False, stop=last, skip_group_check=True)
                op.then_inc(rows_mm, 1)

            def aggregate(g, m, parity, last_group=False):
                p, r, b = m // 2, m % 2, m % NBUF
                if m == 0:
                    pe.wait_ge(x1_split, g + 1)
                by_dve = sum(low_by_dve(k) for k in range(m + 1)) if last_group else 0
                if last_group and low_by_dve(m):
                    pe.wait_ge(nat_lo_dve, by_dve)
                elif last_group:
                    pe.wait_ge(nat_lo_ready, HALVES * g + m + 1 - by_dve)
                else:
                    pe.wait_ge(nat_lo_ready, HALVES * g + m + 1)
                if r == 0:
                    pe.wait_ge(agg_free, CHUNKS * g + p + 1)
                bank = agg_ps[p % 2][:, :]
                pe.matmul(bank, x1_hi[:, parity, r, :], nat_hi[:, b, :], start=r == 0, stop=False)
                pe.matmul(bank, x1_lo[:, parity, r, :], nat_hi[:, b, :], start=False, stop=False)
                pe.matmul(bank, x1_hi[:, parity, r, :], nat_lo[:, b, :], start=False, stop=r == RB - 1)\
                  .then_inc(agg_mm, 1)

            def turn_rows(g):
                pe.wait_ge(rows_sum, g + 1)
                for r in range(RB):
                    op = pe.transpose(norm_ps[:, r * P:(r + 1) * P], turned[:, r * P:(r + 1) * P], ident[:, :])
                op.then_inc(rows_nat, 1)

            def turn_x1(g):
                pe.wait_ge(x1_ready, g)
                for r in range(RB):
                    op = pe.transpose(norm_ps[:, W + r * P:W + (r + 1) * P], x1[:, r, :], ident[:, :])
                op.then_inc(x1_turned, 1)

            def mix_x1(g):
                pe.wait_ge(x1_copied, g)
                pe.wait_ge(xc_ps_read, g)
                for r in range(RB):
                    op = pe.matmul(xc_ps[:, r * P:(r + 1) * P], turned[:, r * P:(r + 1) * P], w_cT[:, :],
                                   start=True, stop=True)
                op.then_inc(xc_mm, 1)

            pe.wait_ge(ident_ready, 1)
            turn(0, 0, 0)
            turn(0, 1, 0)
            pe.wait_ge(small_in, 16 * 5)
            pe.transpose(xc_ps[:, 0:P], xc[:, 0, :], ident[:, :]).then_inc(w_turned, 1)
            for s in range(HALVES + LAG):
                nxt = s + LEAD
                turn(nxt // HALVES, nxt % HALVES, nxt // HALVES)
                if s == 0:
                    pe.wait_ge(xc_ps_read, 1)
                if s < HALVES and s % 2 == 0:
                    pe.wait_ge(x_split, s // 2 + 1)
                rows(s // HALVES, s % HALVES, s // HALVES)
                if s == HALVES:
                    turn_rows(0)

            def group(g, parity):
                for s in range(HALVES):
                    more = not isinstance(g, int) or g < LAST
                    nxt = s + LAG + LEAD
                    if nxt < HALVES:
                        turn(g, nxt, parity)
                    elif more:
                        turn(g + 1, nxt - HALVES, 1 - parity)
                    now = s + LAG
                    if now < HALVES:
                        rows(g, now, parity)
                    elif more:
                        rows(g + 1, now - HALVES, 1 - parity)
                    if s == HALVES - LAG:
                        turn_rows(g)
                    aggregate(g - 1, s, 1 - parity)
                    if s == 0:
                        turn_x1(g)
                    if s == 2:
                        mix_x1(g)

            with pe.Fori(0, (LAST - 1) // 2) as k:
                group(2 * k + 1, 1)
                group(2 * k + 2, 0)
            group(LAST, 1)

            def mix_agg(q):
                c = LAST_ORDER[q]
                pe.wait_ge(agg_free, 2 + CHUNKS * LAST + ORDER.index(c) + 1)
                if q >= 2:
                    pe.wait_ge(h_ready, q - 1)
                for t in range(CT):
                    op = pe.matmul(row_ps[q % 2][:, t * P:(t + 1) * P], agg[:, c, t * P:(t + 1) * P], w_nT,
                                   start=True, stop=True)
                op.then_inc(mix_mm, 1)

            def turn_h(q):
                pe.wait_ge(h_ready, q + 1)
                if q >= 2:
                    pe.wait_ge(hT_ready, q - 1)
                for t in range(CT):
                    op = pe.transpose(turn_ps[q % 2][:, t * P:(t + 1) * P], tail_xc(q)[:, t * P:(t + 1) * P],
                                      ident[:, :])
                op.then_inc(h_turned, 1)

            pe.wait_ge(w_n_here, 16)
            pe.transpose(xc_ps[:, W:W + P], w_n_in, ident[:, :]).then_inc(w_n_turned, 1)
            for p in range(CHUNKS + 4):
                if p == 1:
                    turn_x1(GROUPS)
                if p == 2:
                    pe.wait_ge(w_n_ready, 1)
                    mix_x1(GROUPS)
                if p < CHUNKS:
                    aggregate(LAST, 2 * p, LAST % 2, last_group=True)
                    aggregate(LAST, 2 * p + 1, LAST % 2, last_group=True)
                if 2 <= p < CHUNKS + 2:
                    mix_agg(p - 2)
                if 3 <= p < CHUNKS + 3:
                    turn_h(p - 3)

            for q in range(CHUNKS):
                pe.wait_ge(relu_ready, q + 1)
                if q >= 2:
                    pe.wait_ge(y_ready, q - 1)
                c = LAST_ORDER[q]
                for t in range(CT):
                    op = pe.transpose(row_ps[q % 2][:, t * P:(t + 1) * P], agg[:, c, t * P:(t + 1) * P], ident[:, :])
                op.then_inc(relu_turned, 1)


_INS = ['x', 'adj', 'L0_gnn_h', 'L1_gnn_W_n', 'L1_gnn_b_n', 'L1_gnn_W_c', 'L1_gnn_b_c', 'L1_gnn_gamma',
        'L1_gnn_beta']


def kernel(**inputs):
    import numpy as _np
    import concourse.bacc as _bacc
    from concourse import mybir as _mybir
    from concourse.bass_utils import run_bass_kernel_spmd as _run

    nc = _bacc.Bacc("TRN2", target_bir_lowering=False, num_devices=1, dynamic_dma_scratch_size=2048)
    arrays, args = {}, []
    for name in _INS:
        a = _np.ascontiguousarray(inputs[name])
        arrays[f"in_{name}_dram"] = a
        args.append(nc.dram_tensor(f"in_{name}_dram", a.shape, _mybir.dt.from_np(a.dtype), kind="ExternalInput").ap())
    args.append(nc.dram_tensor("out_0_dram", (N, P), _mybir.dt.float32, kind="ExternalOutput").ap())
    adj_resnorm_kernel(nc, *args)
    r = _run(nc, [arrays], core_ids=[0])
    return r.results[0]["out_0_dram"]
```

```python
import concourse.bass as bass
from concourse import mybir
from contextlib import ExitStack

FP32 = mybir.dt.float32
FP32R = mybir.dt.float32r
ALU = mybir.AluOpType
ACT = mybir.ActivationFunctionType
AX = mybir.AxisListType

P = 128
N = 8192
TILES = N // P
RB = 2
GROUPS = N // (RB * P)
CW = 512
CHUNKS = N // CW
CT = CW // P
HALVES = 2 * CHUNKS
EARLY = 6
SLOTS = CHUNKS + EARLY
QHOMES = 2
Q = 32
LAG = 5
LEAD = 2
ALPHA = 0.1
LN_EPS = 1e-5
BN_EPS = 1e-5
W = RB * P

ORDER = list(range(EARLY, CHUNKS)) + list(range(EARLY))
LAST_ORDER = [c for c in ORDER if c != CHUNKS - 1] + [CHUNKS - 1]
Y_ACT = 1
W_C_STEP = 16
X_RUN = 2
NBUF = 3




def by_vector(g, chunk):
    return chunk % 2 == 1 and not (isinstance(g, int) and g == 0)


def home(chunk, parity):
    return chunk + parity * CHUNKS if chunk < EARLY else chunk


def loads_before(chunk, g):
    return g // 2 + 1 if chunk < EARLY else g + 1


def adj_resnorm_kernel(nc, x, adj, h0, w_n, b_n, w_c, b_c, gamma, beta, out):
    x_v = x.rearrange("(g r p) f -> g p r f", r=RB, p=P)
    x_q = x.rearrange("(c k u) f -> k c (u f)", k=P, u=CT)
    adj_q = adj.rearrange("(g i a) (c q n) -> g c q a i n", a=Q, i=W // Q, q=4, n=P)
    h_v = h0.rearrange("(g r p) f -> g p r f", r=RB, p=P)
    adj_v = adj.rearrange("(g r p) n -> g p r n", r=RB, p=P)
    out_v = out.rearrange("(t p) f -> p t f", p=P)
    x1_dram = nc.dram_tensor("x1_scratch", (P, N), FP32, kind="Internal").ap()
    xc_dram = nc.dram_tensor("xc_scratch", (P, N), FP32, kind="Internal").ap()

    with ExitStack() as ctx:
        def sb(name, shape, dt=FP32):
            return ctx.enter_context(nc.sbuf_tensor(name, shape, dt))

        def pb(name):
            return ctx.enter_context(nc.psum_tensor(name, [P, CW], FP32))

        def sem(name):
            return ctx.enter_context(nc.semaphore(name))

        ring = sb("ring", [P, SLOTS + QHOMES, RB, CW])
        x_hi = sb("x_hi", [P, TILES, P], FP32R)
        x_lo = sb("x_lo", [P, TILES, P], FP32R)
        agg = sb("agg", [P, CHUNKS, CW])
        adjT = sb("adjT", [P, 2, 2, 2, W], FP32R)
        nat_hi = sb("nat_hi", [P, NBUF, CW], FP32R)
        nat_lo = sb("nat_lo", [P, NBUF, CW], FP32R)
        x1_hi = sb("x1_hi", [P, 2, RB, P], FP32R)
        x1_lo = sb("x1_lo", [P, 2, RB, P], FP32R)
        x1 = sb("x1", [P, RB, P])
        turned = sb("turned", [P, W])
        xc = sb("xc", [P, RB, P])
        hx = sb("hx", [P, RB, P])
        w_cT = sb("w_cT", [P, P])
        ident = sb("ident", [P, P])
        part_deg = sb("part_deg", [P, 2, RB, CHUNKS])
        deg = sb("deg", [P, TILES])
        stats = sb("stats", [P, CT, 6])
        mv = sb("mv", [P, CT, 2])
        std = sb("std", [P, RB])
        bn_mv = sb("bn_mv", [P, 2])
        bn_scale = sb("bn_scale", [P, 1])
        bn_shift = sb("bn_shift", [P, 1])
        by_feature = sb("by_feature", [P, 4])
        bn_parts = ring[:, SLOTS, 0, 0:CHUNKS * 6].rearrange("p (c s) -> p c s", s=6)
        no_deg = ring[:, SLOTS + 1, 0, 0:TILES]
        scale_y = ring[:, SLOTS, 1, 0:2 * CT].rearrange("p (b t) -> p b t", t=CT)
        shift_y = ring[:, SLOTS + 1, 1, 0:2 * CT].rearrange("p (b t) -> p b t", t=CT)
        w_n_in, w_nT = hx[:, 0, :], hx[:, 1, :]
        eps = sb("eps", [P, 1])
        assert LN_EPS == BN_EPS

        turn_ps = [pb("turn_ps0"), pb("turn_ps1")]
        row_ps = [pb("row_ps0"), pb("row_ps1")]
        agg_ps = [pb("agg_ps0"), pb("agg_ps1")]
        norm_ps = pb("norm_ps")
        xc_ps = pb("xc_ps")

        chunk_in = [sem(f"chunk_in{s}") for s in range(SLOTS)]
        quarter_in = [sem(f"quarter_in{s}") for s in range(QHOMES)]
        x_in = [sem(f"x_in{s}") for s in range(CHUNKS // X_RUN)]
        small_in = sem("small_in")
        res_in = sem("res_in")
        w_n_here = sem("w_n_here")
        w_n_turned = sem("w_n_turned")
        w_n_ready = sem("w_n_ready")
        h_in = sem("h_in")
        x1_out = sem("x1_out")
        xc_out = sem("xc_out")
        tail_in = [sem(f"tail_in{q}") for q in range(CHUNKS)]
        rows_out = sem("rows_out")
        ident_zero = sem("ident_zero")
        ident_ready = sem("ident_ready")
        w_turned = sem("w_turned")
        bias_ready = sem("bias_ready")
        eps_ready = sem("eps_ready")
        x_hi_ready = sem("x_hi_ready")
        x_split = sem("x_split")
        turned_ps = sem("turned_ps")
        turned_dve = sem("turned_dve")
        adjT_hi = sem("adjT_hi")
        adjT_lo = sem("adjT_lo")
        rows_mm = sem("rows_mm")
        nat_hi_ready = sem("nat_hi_ready")
        nat_lo_ready = sem("nat_lo_ready")
        nat_lo_dve = sem("nat_lo_dve")
        agg_mm = sem("agg_mm")
        agg_free = sem("agg_free")
        half_rows = sem("half_rows")
        rows_sum = sem("rows_sum")
        rows_nat = sem("rows_nat")
        hx_step = sem("hx_step")
        pre_ready = sem("pre_ready")
        norm_step = sem("norm_step")
        mv_ready = sem("mv_ready")
        std_ready = sem("std_ready")
        x1_ready = sem("x1_ready")
        x1_hi_ready = sem("x1_hi_ready")
        x1_split = sem("x1_split")
        x1_turned = sem("x1_turned")
        x1_copied = sem("x1_copied")
        xc_mm = sem("xc_mm")
        xc_ps_read = sem("xc_ps_read")
        deg_ready = sem("deg_ready")
        deg_step = sem("deg_step")
        mix_mm = sem("mix_mm")
        h_ready = sem("h_ready")
        h_turned = sem("h_turned")
        hT_ready = sem("hT_ready")
        bn_part = sem("bn_part")
        bn_step = sem("bn_step")
        bn_std = sem("bn_std")
        relu_ready = sem("relu_ready")
        relu_turned = sem("relu_turned")
        y_ready = sem("y_ready")
        y_step = sem("y_step")
        y_mv = sem("y_mv")
        y_std = sem("y_std")
        y_rstd = sem("y_rstd")
        y_shift = sem("y_shift")
        y_out_act = sem("y_out_act")
        y_out_pool = sem("y_out_pool")

        block = ctx.enter_context(nc.Block())

        LAST = GROUPS - 1
        X_SLOT = CHUNKS
        assert (EARLY + QHOMES) * RB * CW == TILES * P

        def x_staged(chunk):
            half = ring[:, X_SLOT + chunk // 2, chunk % 2, :]
            return half.rearrange("p (t f) -> p t f", f=P)

        def quarters(h):
            return ring[:, SLOTS + h, :, :].rearrange("p r n -> p (r n)").rearrange("p (i n) -> p i n", n=P)

        def turn_bank(g, idx):
            if isinstance(g, int) and g == 0:
                return (turn_ps + agg_ps)[idx % 4]
            return turn_ps[idx % 2]

        def turns_before(g, chunk):
            if isinstance(g, int) and g == 0:
                return 2 * chunk
            if by_vector(g, chunk):
                return CHUNKS * (g - 1) + chunk - 1
            return HALVES + CHUNKS * (g - 1) + chunk

        def low_by_dve(m):
            return m % 8 == 5

        def low_by_dve_until(p):
            return sum(low_by_dve(m) for m in range(2 * p + 2))

        def tail_home(q):
            return home(q, (LAST + 1) % 2) if q < EARLY else home(ORDER[q - EARLY], LAST % 2)

        def tail_x1(q):
            return ring[:, tail_home(q), 0, :]

        def tail_xc(q):
            return ring[:, tail_home(q), 1, :]

        @block.sync
        def _(sp):
            def load_chunk(g, chunk, parity):
                cols = slice(chunk * CW, (chunk + 1) * CW)
                src = adj_v[g, :, :, cols] if isinstance(g, int) else adj_v[bass.ds(g, 1), :, :, cols].squeeze(0)
                slot = home(chunk, parity)
                sp.dma_start(ring[:, slot, :, :], src).then_inc(chunk_in[slot], 16)

            def load_quarters(g, chunk):
                h = chunk // 2 % QHOMES
                for q in range(4):
                    src = adj_q[g, chunk, q] if isinstance(g, int) else \
                        adj_q[bass.ds(g, 1), chunk, q, :, :, :].squeeze(0)
                    sp.dma_start(quarters(h)[q * Q:(q + 1) * Q, :, :], src).then_inc(quarter_in[h], 16)

            def load_residual(g):
                src = x_v[g] if isinstance(g, int) else x_v[bass.ds(g, 1), :, :, :].squeeze(0)
                sp.dma_start(xc[:, :, :], src).then_inc(res_in, 16)

            staged = ring[:, X_SLOT:, :, :].rearrange("p s r n -> p (s r) n")

            def load_x(i):
                run = slice(i * X_RUN, (i + 1) * X_RUN)
                sp.dma_start(staged[:, run, :], x_q[:, run, :]).then_inc(x_in[i], 16)

            for c in range(7):
                load_chunk(0, c, 0)
                if c % X_RUN == 0:
                    load_x(c // X_RUN)
            sp.dma_start(xc[:, 0, :], w_c).then_inc(small_in, 16)
            for i, v in enumerate((gamma, beta, b_n, b_c)):
                sp.dma_start(by_feature[:, i:i + 1], v.rearrange("(p a) -> p a", a=1)).then_inc(small_in, 16)
            sp.dma_start(hx[:, :, :], h_v[0]).then_inc(h_in, 16)
            for c in range(7, CHUNKS):
                load_chunk(0, c, 0)
                if c % X_RUN == 0:
                    load_x(c // X_RUN)
                if c == 12:
                    sp.wait_ge(w_turned, 1)
                    load_residual(0)
            for c in range(EARLY):
                sp.wait_ge(x_split, 2 * c + 2)
                load_chunk(1, c, 1)
            for n, c in enumerate((1, 3, 5)):
                if n < QHOMES:
                    sp.wait_ge(x_split, 2 * (EARLY + n) + 2)
                else:
                    sp.wait_ge(turned_dve, 2)
                load_quarters(1, c)

            def freed(g, p):
                sp.wait_ge(nat_lo_ready, HALVES * (g - 1) + 2 * p + 2)

            def small_traffic(g, p):
                if p == 0:
                    sp.wait_ge(x1_ready, g)
                    sp.dma_start(x1_dram[:, bass.ds((g - 1) * W, W)], x1[:, :, :].rearrange("p r f -> p (r f)"))\
                      .then_inc(x1_out, 16)
                if p == 3:
                    sp.wait_ge(xc_ps_read, g + 1)
                    sp.dma_start(xc_dram[:, bass.ds((g - 1) * W, W)], xc[:, :, :].rearrange("p r f -> p (r f)"))\
                      .then_inc(xc_out, 16)

            def load_h(g):
                sp.wait_ge(pre_ready, g)
                src = h_v[g] if isinstance(g, int) else h_v[bass.ds(g, 1), :, :, :].squeeze(0)
                sp.dma_start(hx[:, :, :], src).then_inc(h_in, 16)

            def group(g, parity):
                for p in range(CHUNKS):
                    freed(g, p)
                    if p < CHUNKS - EARLY:
                        load_chunk(g, ORDER[p], parity)
                    elif not isinstance(g, int) or g < LAST:
                        load_chunk(g + 1, ORDER[p], 1 - parity)
                    if p % 2 == 0:
                        n, c = p // 2 + 3, p + 7
                        if c < CHUNKS:
                            sp.wait_ge(turned_dve, CHUNKS * (g - 1) + 2 * n - 2)
                            load_quarters(g, c)
                        elif not isinstance(g, int) or g < LAST:
                            sp.wait_ge(turned_dve, CHUNKS * (g - 1) + 2 * n - 2)
                            load_quarters(g + 1, c - CHUNKS)
                    small_traffic(g, p)
                    if p == 0:
                        load_h(g)
                    if p == 6:
                        sp.wait_ge(xc_out, 16 * g)
                        load_residual(g)

            with sp.Fori(0, (LAST - 1) // 2) as k:
                group(2 * k + 1, 1)
                group(2 * k + 2, 0)
            group(LAST, 1)

            sp.wait_ge(pre_ready, GROUPS)
            sp.dma_start(w_n_in, w_n).then_inc(w_n_here, 16)
            small_traffic(GROUPS, 0)
            sp.wait_ge(xc_out, 16 * LAST)
            for q in range(CHUNKS):
                if q == EARLY:
                    small_traffic(GROUPS, 3)
                if q == CHUNKS - 1:
                    sp.wait_ge(x1_out, 16 * GROUPS)
                    sp.wait_ge(xc_out, 16 * GROUPS)
                if q >= EARLY:
                    by_dve = low_by_dve_until(q - EARLY)
                    sp.wait_ge(nat_lo_ready, HALVES * LAST + 2 * (q - EARLY + 1) - by_dve)
                    if by_dve:
                        sp.wait_ge(nat_lo_dve, by_dve)
                cols = slice(LAST_ORDER[q] * CW, (LAST_ORDER[q] + 1) * CW)
                sp.dma_start(tail_x1(q), x1_dram[:, cols]).then_inc(tail_in[q], 16)
                sp.dma_start(tail_xc(q), xc_dram[:, cols]).then_inc(tail_in[q], 16)
            for q in range(CHUNKS):
                sp.wait_ge(y_out_act, q + 1)
                sp.wait_ge(y_out_pool, q + 1)
                c = LAST_ORDER[q]
                sp.dma_start(out_v[:, c * CT:(c + 1) * CT, :],
                             tail_x1(q).rearrange("p (t f) -> p t f", f=P)).then_inc(rows_out, 16)
            sp.wait_ge(rows_out, 16 * CHUNKS)

        @block.gpsimd
        def _(pool):
            pool.memset(ident[:, :], 0.0).then_inc(ident_zero, 1)
            pool.wait_ge(ident_zero, 1)
            pool.affine_select(out=ident[:, :], in_=ident[:, :], compare_op=ALU.not_equal, fill=1.0,
                               base=0, pattern=[[-1, P]], channel_multiplier=1).then_inc(ident_ready, 1)
            for c in range(CHUNKS):
                tiles = slice(c * CT, (c + 1) * CT)
                pool.wait_ge(x_hi_ready, c + 1)
                pool.tensor_tensor(x_lo[:, tiles, :], x_staged(c), x_hi[:, tiles, :].bitcast(FP32),
                                   ALU.subtract).then_inc(x_split, 1)
            for i in range(2):
                pool.memset(agg[:, i * CHUNKS // 2:(i + 1) * CHUNKS // 2, :], 0.0).then_inc(agg_free, 1)

            def low_part(g, m, parity):
                slot, r, b = home(ORDER[m // 2], parity), m % 2, m % NBUF
                pool.wait_ge(nat_hi_ready, HALVES * g + m + 1)
                pool.tensor_tensor(nat_lo[:, b, :], ring[:, slot, r, :], nat_hi[:, b, :].bitcast(FP32),
                                   ALU.subtract).then_inc(nat_lo_ready, 1)

            for m in range(LEAD):
                low_part(0, m, 0)

            def group(g, parity):
                for s in range(HALVES):
                    m = s + LEAD
                    if m < HALVES:
                        low_part(g - 1, m, 1 - parity)
                    else:
                        low_part(g, m - HALVES, parity)

            with pool.Fori(0, (LAST - 1) // 2) as k:
                group(2 * k + 1, 1)
                group(2 * k + 2, 0)
            for m in range(LEAD, HALVES):
                low_part(LAST - 1, m, 0)
            for m in range(HALVES):
                if not low_by_dve(m):
                    low_part(LAST, m, LAST % 2)
            for q in range(CHUNKS):
                pool.wait_ge(y_shift, q + 1)
                for t in range(Y_ACT, CT):
                    cols = slice(t * P, (t + 1) * P)
                    op = pool.tensor_scalar(tail_x1(q)[:, cols], tail_x1(q)[:, cols], scale_y[:, q % 2, t:t + 1],
                                            shift_y[:, q % 2, t:t + 1], ALU.mult, ALU.add)
                op.then_inc(y_out_pool, 1)

        @block.scalar
        def _(act):
            def turn_high(g, idx):
                act.wait_ge(turned_dve if by_vector(g, idx // 2) else turned_ps,
                            turns_before(g, idx // 2) + idx % 2 + 1)
                if not (isinstance(g, int) and g == 0 and idx < 2):
                    act.wait_ge(rows_mm, HALVES * g + idx - 1)
                act.activation(adjT[:, idx % 2, :, 0, :],
                               turn_bank(g, idx)[:, :].rearrange("p (t w) -> p t w", w=W), ACT.Copy)\
                   .then_inc(adjT_hi, 1)

            def nat_high(g, m, parity, first=False):
                slot, r, b = home(ORDER[m // 2], parity), m % 2, m % NBUF
                if m >= NBUF:
                    act.wait_ge(agg_mm, HALVES * g + m - NBUF + 1)
                elif m < LEAD and not first:
                    act.wait_ge(agg_mm, HALVES * (g - 1) + HALVES - 1 + m)
                    if m == 0:
                        act.wait_ge(deg_ready, g)
                act.activation(nat_hi[:, b, :], ring[:, slot, r, :], ACT.Copy,
                               accum_out=part_deg[:, parity, r, m // 2:m // 2 + 1]).then_inc(nat_hi_ready, 1)

            def half_of_rows(g, parity):
                act.wait_ge(rows_mm, HALVES * (g + 1))
                if not (isinstance(g, int) and g == 0):
                    act.wait_ge(xc_mm, g)
                act.activation(turned[:, :], row_ps[parity][:, W:2 * W], ACT.Copy).then_inc(half_rows, 1)

            def row_std(g):
                act.wait_ge(mv_ready, RB * (g + 1))
                act.activation(std[:, 0:RB], mv[:, 0:RB, 1], ACT.Sqrt, bias=eps[:, 0:1]).then_inc(std_ready, 1)

            def high_x1(g, parity):
                act.wait_ge(x1_ready, g + 1)
                act.activation(x1_hi[:, parity, :, :], x1[:, :, :], ACT.Copy).then_inc(x1_hi_ready, 1)

            def copy_x1T(g):
                act.wait_ge(x1_turned, g)
                act.activation(turned[:, :], norm_ps[:, W:2 * W], ACT.Copy).then_inc(x1_copied, 1)

            act.wait_ge(eps_ready, 1)
            for s in range(HALVES + LAG + LEAD):
                if s == HALVES + LEAD + 2:
                    row_std(0)
                if s == HALVES + LEAD + 4:
                    high_x1(0, 0)
                turn_high(s // HALVES, s % HALVES)
                if s >= HALVES + LAG:
                    nat_high(0, s - HALVES - LAG, 0, first=True)
                if s == HALVES + LEAD - 1:
                    half_of_rows(0, 0)

            def group(g, parity):
                for s in range(HALVES):
                    if s == 1:
                        copy_x1T(g)
                    m = s + LEAD
                    if m < HALVES:
                        nat_high(g - 1, m, 1 - parity)
                    idx = s + LAG + LEAD
                    if idx < HALVES:
                        turn_high(g, idx)
                    elif not isinstance(g, int) or g < LAST:
                        turn_high(g + 1, idx - HALVES)
                    if s == HALVES - LAG + 2:
                        row_std(g)
                    if m >= HALVES:
                        nat_high(g, m - HALVES, parity)
                    if s == HALVES - LAG + 3:
                        high_x1(g, parity)
                    if s == HALVES - LAG - 1:
                        half_of_rows(g, parity)

            with act.Fori(0, (LAST - 1) // 2) as k:
                group(2 * k + 1, 1)
                group(2 * k + 2, 0)
            group(LAST, 1)

            def copy_hT(q):
                act.wait_ge(h_turned, q + 1)
                act.activation(agg[:, LAST_ORDER[q], :], turn_ps[q % 2][:, :], ACT.Identity,
                               bias=by_feature[:, 2:3]).then_inc(hT_ready, 1)

            act.wait_ge(bias_ready, 1)
            for p in range(CHUNKS + 4):
                if p == 1:
                    copy_x1T(GROUPS)
                for m in (2 * p + LEAD, 2 * p + LEAD + 1):
                    if m < HALVES:
                        nat_high(LAST, m, 1)
                if p >= 4:
                    copy_hT(p - 4)
            act.wait_ge(bn_step, 1)
            act.activation(bn_scale[:, :], bn_mv[:, 1:2], ACT.Sqrt, bias=eps[:, 0:1]).then_inc(bn_std, 1)
            act.wait_ge(bn_step, 5)
            def relu_bn(q):
                c = LAST_ORDER[q]
                act.activation(agg[:, c, :], agg[:, c, :], ACT.Relu, scale=bn_scale[:, 0:1],
                               bias=bn_shift[:, 0:1]).then_inc(relu_ready, 1)

            def y_deviation(q):
                act.wait_ge(y_mv, q + 1)
                if q >= 2:
                    act.wait_ge(y_out_pool, q - 1)
                    act.wait_ge(y_out_act, q - 1)
                act.activation(scale_y[:, q % 2, :], mv[:, :, 1], ACT.Sqrt, bias=eps[:, 0:1]).then_inc(y_std, 1)

            def scale_rows(q):
                act.wait_ge(y_shift, q + 1)
                for t in range(Y_ACT):
                    cols = slice(t * P, (t + 1) * P)
                    op = act.activation(tail_x1(q)[:, cols], tail_x1(q)[:, cols], ACT.Identity,
                                        scale=scale_y[:, q % 2, t:t + 1], bias=shift_y[:, q % 2, t:t + 1])
                op.then_inc(y_out_act, 1)

            relu_bn(0)
            relu_bn(1)
            for q in range(CHUNKS + 1):
                if q + 2 < CHUNKS:
                    relu_bn(q + 2)
                if q < CHUNKS:
                    y_deviation(q)
                if q >= 1:
                    scale_rows(q - 1)

        @block.vector
        def _(dve):
            dve.memset(deg[:, :], 0.0).then_inc(deg_ready, 1)
            dve.memset(eps[:, :], LN_EPS).then_inc(eps_ready, 1)

            def turn_quarters(g, idx):
                chunk, half = idx // 2, idx % 2
                h = chunk // 2 % QHOMES
                if half == 0:
                    dve.wait_ge(quarter_in[h], 64 * (4 * (g - 1) + chunk // 4 + 1))
                dve.wait_ge(adjT_lo, HALVES * g + idx - 1)
                for t in range(2):
                    u = 2 * half + t
                    op = dve.transpose(turn_bank(g, idx)[:, t * W:(t + 1) * W], quarters(h)[:, :, u::CT])
                op.then_inc(turned_dve, 1)

            def turn_low(g, idx):
                dve.wait_ge(adjT_hi, HALVES * g + idx + 1)
                dve.tensor_tensor(adjT[:, idx % 2, :, 1, :],
                                  turn_bank(g, idx)[:, :].rearrange("p (t w) -> p t w", w=W),
                                  adjT[:, idx % 2, :, 0, :].bitcast(FP32), ALU.subtract).then_inc(adjT_lo, 1)

            def add_agg(g, p):
                dve.wait_ge(agg_mm, HALVES * g + 2 * p + 2)
                c = ORDER[p]
                dve.tensor_tensor(agg[:, c, :], agg_ps[p % 2][:, :], agg[:, c, :], ALU.add).then_inc(agg_free, 1)

            def add_hx(g):
                dve.wait_ge(h_in, 16 * (g + 1))
                dve.wait_ge(res_in, 16 * (g + 1))
                dve.scalar_tensor_tensor(hx[:, :, :], hx[:, :, :], ALPHA, xc[:, :, :], ALU.mult, ALU.add)\
                   .then_inc(hx_step, 1)

            def sum_rows(g, parity):
                dve.wait_ge(half_rows, g + 1)
                dve.tensor_tensor(turned[:, :], row_ps[parity][:, 0:W], turned[:, :], ALU.add)\
                   .then_inc(rows_sum, 1)

            def row_stats(g):
                dve.wait_ge(rows_nat, g + 1)
                dve.wait_ge(hx_step, g + 1)
                if not (isinstance(g, int) and g == 0):
                    dve.wait_ge(x1_out, 16 * g)
                    dve.wait_ge(x1_turned, g)
                dve.scalar_tensor_tensor(x1[:, :, :].rearrange("p r f -> p (r f)"), norm_ps[:, 0:W], 1.0 - ALPHA,
                                         hx[:, :, :].rearrange("p r f -> p (r f)"), ALU.mult, ALU.add)\
                   .then_inc(pre_ready, 1)
                dve.wait_ge(pre_ready, g + 1)
                for r in range(RB):
                    dve.bn_stats(stats[:, r, :], x1[:, r, :]).then_inc(norm_step, 1)

            def row_aggr(g):
                for r in range(RB):
                    dve.bn_aggr(mv[:, r, :], stats[:, r, :]).then_inc(mv_ready, 1)

            def invert_std(g):
                dve.wait_ge(std_ready, g + 1)
                dve.reciprocal(std[:, 0:RB], std[:, 0:RB]).then_inc(norm_step, 1)

            def normalise(g):
                dve.wait_ge(norm_step, 3 * g + 3)
                for r in range(RB):
                    op = dve.tensor_scalar(x1[:, r, :], x1[:, r, :], mv[:, r, 0:1], std[:, r:r + 1],
                                           ALU.subtract, ALU.mult)
                op.then_inc(x1_ready, 1)

            def low_x1(g, parity):
                dve.wait_ge(x1_hi_ready, g + 1)
                dve.tensor_tensor(x1_lo[:, parity, :, :], x1[:, :, :], x1_hi[:, parity, :, :].bitcast(FP32),
                                  ALU.subtract).then_inc(x1_split, 1)

            def copy_xc(g):
                dve.wait_ge(xc_mm, g)
                dve.tensor_copy(xc[:, :, :], xc_ps[:, 0:W].rearrange("p (r f) -> p r f", f=P))\
                   .then_inc(xc_ps_read, 1)

            def sum_deg(g, parity):
                dve.wait_ge(nat_hi_ready, HALVES * g)
                tiles = slice((g - 1) * RB, g * RB) if isinstance(g, int) else bass.ds((g - 1) * RB, RB)
                dve.reduce_sum(deg[:, tiles], part_deg[:, 1 - parity, :, :], AX.X).then_inc(deg_ready, 1)

            def high_x(c):
                dve.wait_ge(x_in[c // X_RUN], 16)
                dve.tensor_copy(x_hi[:, c * CT:(c + 1) * CT, :], x_staged(c)).then_inc(x_hi_ready, 1)

            high_x(0)
            for s in range(HALVES + LAG + LEAD):
                if s == W_C_STEP + 1:
                    dve.wait_ge(small_in, 16 * 5)
                    dve.tensor_tensor(by_feature[:, 2:3], by_feature[:, 2:3], by_feature[:, 3:4], ALU.add)\
                       .then_inc(bias_ready, 1)
                    dve.wait_ge(w_turned, 1)
                    dve.tensor_copy(w_cT[:, :], xc_ps[:, 0:P]).then_inc(xc_ps_read, 1)
                if s == HALVES - 8:
                    add_hx(0)
                nxt = s + 1
                if nxt < HALVES + LAG + LEAD + 1 and by_vector(nxt // HALVES, nxt % HALVES // 2):
                    turn_quarters(nxt // HALVES, nxt % HALVES)
                if s == HALVES + LEAD + 1:
                    dve.wait_ge(norm_step, 2)
                turn_low(s // HALVES, s % HALVES)
                if s % 2 == 0 and s // 2 + 1 < CHUNKS:
                    high_x(s // 2 + 1)
                if s == HALVES + LEAD - 1:
                    sum_rows(0, 0)
                if s == HALVES + LEAD:
                    row_stats(0)
                if s == HALVES + LEAD + 1:
                    row_aggr(0)
                if s == HALVES + LEAD + 2:
                    invert_std(0)
                    normalise(0)
                if s == HALVES + LEAD + 3:
                    low_x1(0, 0)

            def turn_ahead(g, s):
                nxt = s + LAG + LEAD + 1
                if nxt < HALVES:
                    if by_vector(g, nxt // 2):
                        turn_quarters(g, nxt)
                elif (not isinstance(g, int) or g < LAST) and by_vector(g + 1, (nxt - HALVES) // 2):
                    turn_quarters(g + 1, nxt - HALVES)

            def low(g, s):
                idx = s + LAG + LEAD
                if idx < HALVES:
                    turn_low(g, idx)
                elif not isinstance(g, int) or g < LAST:
                    turn_low(g + 1, idx - HALVES)

            def group(g, parity):
                for s in range(HALVES):
                    if s == 4:
                        copy_xc(g)
                    if s == HALVES - 12:
                        add_hx(g)
                    turn_ahead(g, s)
                    if s == HALVES - LAG + 1:
                        dve.wait_ge(norm_step, 3 * g + 2)
                    low(g, s)
                    if s == HALVES - LAG:
                        row_stats(g)
                    if s == HALVES - LAG + 2:
                        invert_std(g)
                    if s % 2 == 1:
                        add_agg(g - 1, s // 2)
                    if s == HALVES - LAG - 1:
                        sum_rows(g, parity)
                    if s == HALVES - LAG + 1:
                        row_aggr(g)
                    if s == HALVES - LAG + 2:
                        normalise(g)
                    if s == HALVES - LAG + 3:
                        low_x1(g, parity)
                sum_deg(g, parity)

            with dve.Fori(0, (LAST - 1) // 2) as k:
                group(2 * k + 1, 1)
                group(2 * k + 2, 0)
            group(LAST, 1)

            steps = [0]

            def invert_deg(cols):
                d = deg[:, cols]
                z = no_deg[:, cols]
                dve.tensor_scalar(z, d, 0.0, None, ALU.is_equal).then_inc(deg_step, 1)
                dve.wait_ge(deg_step, steps[0] + 1)
                dve.tensor_tensor(d, d, z, ALU.add).then_inc(deg_step, 1)
                dve.wait_ge(deg_step, steps[0] + 2)
                dve.reciprocal(d, d).then_inc(deg_step, 1)
                dve.wait_ge(deg_step, steps[0] + 3)
                steps[0] += 3

            def h_rows(q):
                c = LAST_ORDER[q]
                dve.wait_ge(mix_mm, q + 1)
                dve.wait_ge(tail_in[q], 32)
                for t in range(CT):
                    cols = slice(t * P, (t + 1) * P)
                    op = dve.scalar_tensor_tensor(tail_xc(q)[:, cols], row_ps[q % 2][:, cols],
                                                  deg[:, c * CT + t:c * CT + t + 1], tail_xc(q)[:, cols],
                                                  ALU.mult, ALU.add)
                op.then_inc(h_ready, 1)

            def bn_part_of(q):
                dve.wait_ge(hT_ready, q + 1)
                dve.bn_stats(bn_parts[:, q, :], agg[:, LAST_ORDER[q], :]).then_inc(bn_part, 1)

            dve.wait_ge(deg_ready, 1 + LAST)
            invert_deg(slice(0, TILES - RB))
            for p in range(CHUNKS + 4):
                if p == 0:
                    dve.wait_ge(w_n_turned, 1)
                    dve.tensor_copy(w_nT, xc_ps[:, W:W + P]).then_inc(w_n_ready, 1)
                for m in (2 * p, 2 * p + 1):
                    if m < HALVES and low_by_dve(m):
                        slot, b = home(ORDER[p], LAST % 2), m % NBUF
                        dve.wait_ge(nat_hi_ready, HALVES * LAST + m + 1)
                        dve.tensor_tensor(nat_lo[:, b, :], ring[:, slot, m % 2, :], nat_hi[:, b, :].bitcast(FP32),
                                          ALU.subtract).then_inc(nat_lo_dve, 1)
                if 1 <= p <= CHUNKS:
                    add_agg(LAST, p - 1)
                if p == CHUNKS:
                    sum_deg(GROUPS, GROUPS % 2)
                    dve.wait_ge(deg_ready, 1 + GROUPS)
                    invert_deg(slice(TILES - RB, TILES))
                if p == 2:
                    copy_xc(GROUPS)
                if 3 <= p < CHUNKS + 3:
                    h_rows(p - 3)
                if p >= 4:
                    bn_part_of(p - 4)

            dve.wait_ge(bn_part, CHUNKS)
            dve.bn_aggr(bn_mv[:, :], bn_parts[:, :, :]).then_inc(bn_step, 1)
            dve.wait_ge(bn_std, 1)
            dve.reciprocal(bn_scale[:, :], bn_scale[:, :]).then_inc(bn_step, 1)
            dve.wait_ge(bn_step, 2)
            dve.tensor_tensor(bn_scale[:, :], bn_scale[:, :], by_feature[:, 0:1], ALU.mult).then_inc(bn_step, 1)
            dve.wait_ge(bn_step, 3)
            dve.tensor_tensor(bn_shift[:, :], bn_mv[:, 0:1], bn_scale[:, :], ALU.mult).then_inc(bn_step, 1)
            dve.wait_ge(bn_step, 4)
            dve.tensor_tensor(bn_shift[:, :], by_feature[:, 1:2], bn_shift[:, :], ALU.subtract).then_inc(bn_step, 1)

            def invert_y_std(q):
                dve.wait_ge(y_std, q + 1)
                dve.reciprocal(scale_y[:, q % 2, :], scale_y[:, q % 2, :]).then_inc(y_rstd, 1)

            def shift_rows(q):
                dve.wait_ge(y_rstd, q + 1)
                if q >= 2:
                    dve.wait_ge(y_out_pool, q - 1)
                    dve.wait_ge(y_out_act, q - 1)
                dve.scalar_tensor_tensor(shift_y[:, q % 2, :], mv[:, :, 0], -1.0, scale_y[:, q % 2, :],
                                         ALU.mult, ALU.mult).then_inc(y_shift, 1)

            for q in range(CHUNKS):
                dve.wait_ge(relu_turned, q + 1)
                dve.tensor_tensor(tail_x1(q), row_ps[q % 2][:, :], tail_x1(q), ALU.add).then_inc(y_ready, 1)
                dve.wait_ge(y_ready, q + 1)
                for t in range(CT):
                    if t == CT - 1 and q >= 1:
                        invert_y_std(q - 1)
                    dve.bn_stats(stats[:, t, :], tail_x1(q)[:, t * P:(t + 1) * P]).then_inc(y_step, 1)
                if q >= 1:
                    shift_rows(q - 1)
                    dve.wait_ge(y_shift, q)
                dve.wait_ge(y_step, CT * (q + 1))
                for t in range(CT):
                    op = dve.bn_aggr(mv[:, t, :], stats[:, t, :])
                op.then_inc(y_mv, 1)
            invert_y_std(CHUNKS - 1)
            shift_rows(CHUNKS - 1)

        @block.tensor
        def _(pe):
            def turn(g, idx, parity):
                chunk, half = idx // 2, idx % 2
                if by_vector(g, chunk):
                    return
                slot = home(chunk, parity)
                tiles = ring[:, slot, :, :].rearrange("p r (k u) -> p r u k", u=CT)
                if idx % 2 == 0:
                    if isinstance(g, int):
                        pe.wait_ge(chunk_in[slot], 16 * loads_before(chunk, g))
                    elif chunk < EARLY:
                        pe.wait_ge(chunk_in[slot], (g - parity) * 8 + 16)
                    else:
                        pe.wait_ge(chunk_in[slot], g * 16 + 16)
                if isinstance(g, int) and g == 0:
                    if idx >= 4:
                        pe.wait_ge(adjT_lo, idx - 3)
                else:
                    pe.wait_ge(adjT_lo, HALVES * g + idx - 1)
                for t in range(2):
                    for r in range(RB):
                        op = pe.transpose(turn_bank(g, idx)[:, t * W + r * P:t * W + (r + 1) * P],
                                          tiles[:, r, 2 * half + t, :], ident[:, :])
                op.then_inc(turned_ps, 1)

            def rows(g, idx, parity):
                pe.wait_ge(adjT_lo, HALVES * g + idx + 1)
                if idx == 0 and not (isinstance(g, int) and g < 2):
                    pe.wait_ge(rows_sum, g - 1)
                for t in range(2):
                    tile = 2 * idx + t
                    first, last = idx == 0 and t == 0, idx == HALVES - 1 and t == 1
                    pe.matmul(row_ps[parity][:, :], x_hi[:, tile, :],
                              adjT[:, idx % 2, t, :, :].rearrange("p a w -> p (a w)"), start=first, stop=False,
                              skip_group_check=True)
                    op = pe.matmul(row_ps[parity][:, 0:W], x_lo[:, tile, :], adjT[:, idx % 2, t, 0, :],
                                   start=False, stop=last, skip_group_check=True)
                op.then_inc(rows_mm, 1)

            def aggregate(g, m, parity, last_group=False):
                p, r, b = m // 2, m % 2, m % NBUF
                if m == 0:
                    pe.wait_ge(x1_split, g + 1)
                by_dve = sum(low_by_dve(k) for k in range(m + 1)) if last_group else 0
                if last_group and low_by_dve(m):
                    pe.wait_ge(nat_lo_dve, by_dve)
                elif last_group:
                    pe.wait_ge(nat_lo_ready, HALVES * g + m + 1 - by_dve)
                else:
                    pe.wait_ge(nat_lo_ready, HALVES * g + m + 1)
                if r == 0:
                    pe.wait_ge(agg_free, CHUNKS * g + p + 1)
                bank = agg_ps[p % 2][:, :]
                pe.matmul(bank, x1_hi[:, parity, r, :], nat_hi[:, b, :], start=r == 0, stop=False)
                pe.matmul(bank, x1_lo[:, parity, r, :], nat_hi[:, b, :], start=False, stop=False)
                pe.matmul(bank, x1_hi[:, parity, r, :], nat_lo[:, b, :], start=False, stop=r == RB - 1)\
                  .then_inc(agg_mm, 1)

            def turn_rows(g):
                pe.wait_ge(rows_sum, g + 1)
                for r in range(RB):
                    op = pe.transpose(norm_ps[:, r * P:(r + 1) * P], turned[:, r * P:(r + 1) * P], ident[:, :])
                op.then_inc(rows_nat, 1)

            def turn_x1(g):
                pe.wait_ge(x1_ready, g)
                for r in range(RB):
                    op = pe.transpose(norm_ps[:, W + r * P:W + (r + 1) * P], x1[:, r, :], ident[:, :])
                op.then_inc(x1_turned, 1)

            def mix_x1(g):
                pe.wait_ge(x1_copied, g)
                pe.wait_ge(xc_ps_read, g)
                for r in range(RB):
                    op = pe.matmul(xc_ps[:, r * P:(r + 1) * P], turned[:, r * P:(r + 1) * P], w_cT[:, :],
                                   start=True, stop=True)
                op.then_inc(xc_mm, 1)

            pe.wait_ge(ident_ready, 1)
            for idx in range(LEAD + 1):
                turn(0, idx, 0)
            for s in range(HALVES + LAG):
                if s + LEAD + 1 < HALVES:
                    turn(0, s + LEAD + 1, 0)
                if s + LEAD >= HALVES:
                    turn(1, s + LEAD - HALVES, 1)
                if s == W_C_STEP:
                    pe.wait_ge(small_in, 16 * 5)
                    pe.transpose(xc_ps[:, 0:P], xc[:, 0, :], ident[:, :]).then_inc(w_turned, 1)
                if s < HALVES and s % 2 == 0:
                    pe.wait_ge(x_split, s // 2 + 1)
                rows(s // HALVES, s % HALVES, s // HALVES)
                if s == HALVES:
                    turn_rows(0)

            def group(g, parity):
                for s in range(HALVES):
                    more = not isinstance(g, int) or g < LAST
                    nxt = s + LAG + LEAD
                    if nxt < HALVES:
                        turn(g, nxt, parity)
                    elif more:
                        turn(g + 1, nxt - HALVES, 1 - parity)
                    now = s + LAG
                    if now < HALVES:
                        rows(g, now, parity)
                    elif more:
                        rows(g + 1, now - HALVES, 1 - parity)
                    aggregate(g - 1, s, 1 - parity)
                    if s == HALVES - LAG:
                        turn_rows(g)
                    if s == 0:
                        turn_x1(g)
                    if s == 2:
                        mix_x1(g)

            with pe.Fori(0, (LAST - 1) // 2) as k:
                group(2 * k + 1, 1)
                group(2 * k + 2, 0)
            group(LAST, 1)

            def mix_agg(q):
                c = LAST_ORDER[q]
                pe.wait_ge(agg_free, 2 + CHUNKS * LAST + ORDER.index(c) + 1)
                if q >= 2:
                    pe.wait_ge(h_ready, q - 1)
                for t in range(CT):
                    op = pe.matmul(row_ps[q % 2][:, t * P:(t + 1) * P], agg[:, c, t * P:(t + 1) * P], w_nT,
                                   start=True, stop=True)
                op.then_inc(mix_mm, 1)

            def turn_h(q):
                pe.wait_ge(h_ready, q + 1)
                if q >= 2:
                    pe.wait_ge(hT_ready, q - 1)
                for t in range(CT):
                    op = pe.transpose(turn_ps[q % 2][:, t * P:(t + 1) * P], tail_xc(q)[:, t * P:(t + 1) * P],
                                      ident[:, :])
                op.then_inc(h_turned, 1)

            pe.wait_ge(w_n_here, 16)
            pe.transpose(xc_ps[:, W:W + P], w_n_in, ident[:, :]).then_inc(w_n_turned, 1)
            for p in range(CHUNKS + 4):
                if p == 1:
                    turn_x1(GROUPS)
                if p == 2:
                    pe.wait_ge(w_n_ready, 1)
                    mix_x1(GROUPS)
                if p < CHUNKS:
                    aggregate(LAST, 2 * p, LAST % 2, last_group=True)
                    aggregate(LAST, 2 * p + 1, LAST % 2, last_group=True)
                if 2 <= p < CHUNKS + 2:
                    mix_agg(p - 2)
                if 3 <= p < CHUNKS + 3:
                    turn_h(p - 3)

            for q in range(CHUNKS):
                pe.wait_ge(relu_ready, q + 1)
                if q >= 2:
                    pe.wait_ge(y_ready, q - 1)
                c = LAST_ORDER[q]
                for t in range(CT):
                    op = pe.transpose(row_ps[q % 2][:, t * P:(t + 1) * P], agg[:, c, t * P:(t + 1) * P], ident[:, :])
                op.then_inc(relu_turned, 1)


_INS = ['x', 'adj', 'L0_gnn_h', 'L1_gnn_W_n', 'L1_gnn_b_n', 'L1_gnn_W_c', 'L1_gnn_b_c', 'L1_gnn_gamma',
        'L1_gnn_beta']


def kernel(**inputs):
    import numpy as _np
    import concourse.bacc as _bacc
    from concourse import mybir as _mybir
    from concourse.bass_utils import run_bass_kernel_spmd as _run

    nc = _bacc.Bacc("TRN2", target_bir_lowering=False, num_devices=1, dynamic_dma_scratch_size=2048)
    arrays, args = {}, []
    for name in _INS:
        a = _np.ascontiguousarray(inputs[name])
        arrays[f"in_{name}_dram"] = a
        args.append(nc.dram_tensor(f"in_{name}_dram", a.shape, _mybir.dt.from_np(a.dtype), kind="ExternalInput").ap())
    args.append(nc.dram_tensor("out_0_dram", (N, P), _mybir.dt.float32, kind="ExternalOutput").ap())
    adj_resnorm_kernel(nc, *args)
    r = _run(nc, [arrays], core_ids=[0])
    return r.results[0]["out_0_dram"]
```
